# Optimizing a Trainium2 kernel written in Bass

```python
import numpy as np
import jax
import jax.numpy as jnp

def _softmax(x, axis=-1):
    return jax.nn.softmax(x, axis=axis)

def _gelu(x):
    return jax.nn.gelu(x, approximate=True)

def _silu(x):
    return jax.nn.silu(x)

def _sigmoid(x):
    return jax.nn.sigmoid(x)

def _layernorm(x, axis=-1, eps=1e-05):
    m = jnp.mean(x, axis=axis, keepdims=True)
    v = jnp.var(x, axis=axis, keepdims=True)
    return (x - m) / jnp.sqrt(v + eps)

def _scatter_add(tgt, idx, src, axis=0):
    return tgt.at[idx].add(src)

def _segment_sum(src, seg, n):
    return jax.ops.segment_sum(src, seg, n)
kernel_name = 'mk_xattn_ffn_d1_seqx_r8_bbf4fe'

def setup_inputs(seed: int=0):
    np.random.seed(seed)
    _w = jnp.asarray

    def _rec_inputs():
        import jax
        import jax.numpy as jnp
        _rk = jax.random.key(seed)
        x = 0.5 + 0.2887 * jax.random.normal(jax.random.fold_in(_rk, 1), (4, 256, 256), jnp.float32)
        _lenS = 256 - jax.random.randint(jax.random.fold_in(_rk, 7), (4,), 0, max(1, 256 // 4) + 1, jnp.int32)
        _lenS2 = 256 - jax.random.randint(jax.random.fold_in(_rk, 8), (4,), 0, max(1, 256 // 4) + 1, jnp.int32)
        _ctx_512P = jax.random.normal(jax.random.fold_in(_rk, 11), (4, 16, 64), jnp.float32)
        _ctx_512c = jax.random.dirichlet(jax.random.fold_in(_rk, 511), 0.3 * jnp.ones((16,), jnp.float32), (4, 256))
        _ctx_512t = jnp.einsum('bsk,bkd->bsd', _ctx_512c, _ctx_512P)
        _ctx_512t = _ctx_512t * jax.lax.rsqrt(jnp.mean(jnp.square(_ctx_512t)) + 1e-12) * 0.953939
        ctx_512 = -0.000392918 + 0.999932 * (_ctx_512t + 0.3 * jax.random.normal(jax.random.fold_in(_rk, 611), (4, 256, 64), jnp.float32))
        return (x, ctx_512)
    x, ctx_512 = _rec_inputs()

    def _L0_xattn_setup():
        import jax, jax.numpy as jnp
        import numpy as np
        B, N, D = (16, 256, 64)
        H = 4
        TOP_K_RATIO = 0.3
        key = jax.random.key(seed)
        k1, k2, k3, k4 = jax.random.split(key, 4)
        h = jax.random.normal(k1, (B, N, D), dtype=jnp.float32)
        adj_raw = jax.random.uniform(k2, (B, N, N), dtype=jnp.float32)
        lim = 1.0 / np.sqrt(D)
        Wq = jax.random.uniform(k3, (D, D), minval=-lim, maxval=lim, dtype=jnp.float32)
        Wk = jax.random.uniform(k4, (D, D), minval=-lim, maxval=lim, dtype=jnp.float32)
        gamma_raw = jnp.float32(-0.85)
        return {'h': h, 'adj_raw': adj_raw, 'Wq': Wq, 'Wk': Wk, 'gamma_raw': gamma_raw}
    _L0_xattn_all = _L0_xattn_setup()
    _L0_xattn_in = {k: v for k, v in _L0_xattn_all.items() if k in ('Wq', 'Wk', 'gamma_raw')}
    del _L0_xattn_all

    def _L0_ffn_setup():
        import jax, jax.numpy as jnp
        import numpy as np
        B, S, H, F, E, K = (2, 128, 256, 688, 8, 2)
        key = jax.random.key(seed)
        k0, k1, k2, k3, k4 = jax.random.split(key, 5)
        x = jax.random.normal(k0, (B, S, H), dtype=jnp.float32)
        router_w = jax.random.normal(k1, (E, H), dtype=jnp.float32) * 0.02
        gate_w = jax.random.normal(k2, (E, F, H), dtype=jnp.float32) * 0.02
        up_w = jax.random.normal(k3, (E, F, H), dtype=jnp.float32) * 0.02
        down_w = jax.random.normal(k4, (E, H, F), dtype=jnp.float32) * 0.02
        return {'x': x, 'router_w': router_w, 'gate_w': gate_w, 'up_w': up_w, 'down_w': down_w}
    _L0_ffn_all = _L0_ffn_setup()
    _L0_ffn_in = {k: v for k, v in _L0_ffn_all.items() if k in ('router_w', 'gate_w', 'up_w', 'down_w')}
    del _L0_ffn_all
    return {'x': x, 'ctx_512': ctx_512, 'L0_xattn_Wq': _L0_xattn_in['Wq'], 'L0_xattn_Wk': _L0_xattn_in['Wk'], 'L0_xattn_gamma_raw': _L0_xattn_in['gamma_raw'], 'L0_ffn_router_w': _L0_ffn_in['router_w'], 'L0_ffn_gate_w': _L0_ffn_in['gate_w'], 'L0_ffn_up_w': _L0_ffn_in['up_w'], 'L0_ffn_down_w': _L0_ffn_in['down_w']}

def reference(x, ctx_512, L0_xattn_Wq, L0_xattn_Wk, L0_xattn_gamma_raw, L0_ffn_router_w, L0_ffn_gate_w, L0_ffn_up_w, L0_ffn_down_w):
    import jax
    import jax.numpy as jnp

    def _L0_xattn_ref(h, adj_raw, Wq, Wk, gamma_raw):
        import jax, jax.numpy as jnp
        import numpy as np
        B, N, D = (16, 256, 64)
        H = 4
        TOP_K_RATIO = 0.3
        b, n, dm = h.shape
        d = dm // H
        Q = (h @ Wq.T).reshape(b, n, H, d).transpose(0, 2, 1, 3)
        K = (h @ Wk.T).reshape(b, n, H, d).transpose(0, 2, 1, 3)
        sim = jnp.einsum('bhnd,bhmd->bnm', Q, K) / (jnp.sqrt(jnp.float32(d)) * H)
        k = max(1, int(n * TOP_K_RATIO))
        topk_vals = jax.lax.top_k(sim, k)[0]
        threshold = topk_vals[:, :, -1:]
        sparse_mask = (sim >= threshold).astype(sim.dtype)
        A_learned = jax.nn.sigmoid(sim) * sparse_mask
        A_learned = (A_learned + jnp.swapaxes(A_learned, -1, -2)) * 0.5
        gamma = jax.nn.sigmoid(gamma_raw)
        return (1.0 - gamma) * adj_raw + gamma * A_learned

    def _L0_ffn_ref(x, router_w, gate_w, up_w, down_w):
        import jax, jax.numpy as jnp
        import numpy as np
        B, S, H, F, E, K = (2, 128, 256, 688, 8, 2)
        b, s, h = x.shape
        xf = x.reshape(-1, h)
        logits = xf @ router_w.T
        top_v, top_i = jax.lax.top_k(logits, K)
        probs = jax.nn.softmax(top_v.astype(jnp.float32), axis=-1).astype(logits.dtype)
        combine = jnp.sum(jax.nn.one_hot(top_i, E, dtype=x.dtype) * probs[..., None], axis=1)
        g = jnp.einsum('th,efh->etf', xf, gate_w)
        u = jnp.einsum('th,efh->etf', xf, up_w)
        y = jnp.einsum('etf,ehf->eth', jax.nn.silu(g) * u, down_w)
        out = jnp.einsum('te,eth->th', combine, y)
        return out.reshape(b, s, h)
    x = x + _L0_xattn_ref(ctx_512, _layernorm(x, axis=-1), L0_xattn_Wq, L0_xattn_Wk, L0_xattn_gamma_raw)
    x = x + _L0_ffn_ref(_layernorm(x, axis=-1), L0_ffn_router_w, L0_ffn_gate_w, L0_ffn_up_w, L0_ffn_down_w)
    return x

_drawn_inputs = setup_inputs


def setup_inputs(seed=0):
    import zlib

    import numpy as np

    out = dict(_drawn_inputs(seed))
    spreads = {}
    factors = {'L0_ffn_router_w': 3.702,
     'L0_ffn_gate_w': 3.255,
     'L0_ffn_up_w': 3.23,
     'L0_ffn_down_w': 3.235}
    for name, (base, spread) in spreads.items():
        noise = np.random.default_rng([zlib.crc32(name.encode()), seed]).standard_normal(out[name].shape)
        drawn = base * np.exp(spread * noise) if base else spread * noise
        out[name] = jnp.asarray(drawn.astype(out[name].dtype))
    for name, factor in factors.items():
        out[name] = (out[name] * factor).astype(out[name].dtype)
    return out
```

```python
import concourse.bass as bass
from concourse import mybir
from contextlib import ExitStack

F32 = mybir.dt.float32
F32R = mybir.dt.float32r
F16 = mybir.dt.float16
I32 = mybir.dt.int32
U32 = mybir.dt.uint32
ALU = mybir.AluOpType
ACT = mybir.ActivationFunctionType
AX = mybir.AxisListType

P = 128
B, N, D = 4, 256, 64
H = 256
TOK = B * N
NT = TOK // P
TPB = N // P
KTOP = int(N * 0.3)
ROUNDS = (KTOP + 7) // 8
E, F = 8, 688
KC = H // P
FCH = F // 2
FB = (F + P - 1) // P
FREST = F - (FB - 1) * P
GU_COLS = 2 * KC * F
W_COLS = GU_COLS + FB * H
MAXT = TOK // P
LOG_MAXT = MAXT.bit_length() - 1
EPS = 1e-5
LOWEST = -3.4e38
SKIP = 4096.0
ROW = H + E

GU_PIECES = [(i * F, F) for i in range(2 * KC)]
D_PIECES = [(GU_COLS + i * (FB * H // 2), FB * H // 2) for i in range(2)]
PIECES = GU_PIECES + D_PIECES

SIM = [0, 1, 2, 3]
SUM, XNT, LOG, IDS = 4, 5, 6, 7
GB, UB = [0, 2], [1, 3]
TB = [4, 6]
XB, YB = 5, 7


def after(tiles):
    return tiles + 1


class TileClass:

    def __init__(self, name, sb, sem, gather_slots):
        self.name = name
        self.xg = [sb(f"xg{name}{i}", [P, ROW], F32) for i in range(gather_slots)]
        self.xt_hi = sb(f"xt_hi{name}", [P, KC, P], F32R)
        self.xt_lo = sb(f"xt_lo{name}", [P, KC, P], F32R)
        self.h = sb(f"h{name}", [P, FB * P], F32)
        self.y = sb(f"y{name}", [P, H], F32)
        self.weight = [sb(f"weight{name}{i}", [P, 1], F32) for i in range(gather_slots)]
        self.from_rows = [sb(f"from_rows{name}{i}", [P, 1], U32) for i in range(gather_slots)]
        self.to_rows = sb(f"to_rows{name}", [P, 1], U32)
        self.gathered = [sem(f"gathered{name}{i}") for i in range(gather_slots)]
        self.from_listed = sem(f"from_listed{name}")
        self.to_listed = sem(f"to_listed{name}")
        self.x_transposed = sem(f"x_transposed{name}")
        self.x_hi_ready = sem(f"x_hi_ready{name}")
        self.x_ready = sem(f"x_ready{name}")
        self.weight_ready = sem(f"weight_ready{name}")
        self.gu_done = [sem(f"gu_done{name}{c}") for c in range(2)]
        self.silu_ready = [sem(f"silu_ready{name}{c}") for c in range(2)]
        self.h_ready = [sem(f"h_ready{name}{c}") for c in range(2)]
        self.h_transposed = [sem(f"h_transposed{name}{c}") for c in range(2)]
        self.ht_hi_ready = [sem(f"ht_hi_ready{name}{c}") for c in range(2)]
        self.ht_ready = [sem(f"ht_ready{name}{c}") for c in range(2)]
        self.down_done = sem(f"down_done{name}")
        self.y_ready = sem(f"y_ready{name}")

    def start_counts(self, eng):
        for s in (self.from_listed, self.to_listed, self.x_transposed, self.x_hi_ready, self.x_ready, self.weight_ready,
                  *self.gu_done,
                  *self.silu_ready, *self.h_ready, *self.h_transposed, *self.ht_hi_ready, *self.ht_ready,
                  self.down_done, self.y_ready):
            eng.sem_inc(s, 1)


def xattn_moe_kernel(nc, x, ctxT, wqT, wkT, gamma, routerT, gate, up, down, down_rest, out):
    scratch = nc.dram_tensor("xn_rows", (TOK, ROW), F32, kind="Internal").ap()
    x_view = x.rearrange("b (r p) d -> p (b r) d", p=P)
    out_view = out.rearrange("b (r p) d -> p (b r) d", p=P)
    out_rows = out.rearrange("b n d -> (b n) d")
    scratch_view = scratch.rearrange("(j p) d -> p j d", p=P)

    ctx = ExitStack()
    with ctx:
        def sb(name, shape, dt):
            return ctx.enter_context(nc.sbuf_tensor(name, shape, dt))

        def sem(name):
            return ctx.enter_context(nc.semaphore(name))

        ps = ctx.enter_context(nc.psum_tensor("ps", [P, 8, 512], F32))

        xs = sb("xs", [P, NT, H], F32)
        x2 = sb("x2", [P, NT, H], F32)
        xn = sb("xn", [P, NT, ROW], F32)
        ctx_sb = sb("ctx_sb", [D, TOK], F32)
        wq_sb = sb("wq_sb", [D, D], F32)
        wk_sb = sb("wk_sb", [D, D], F32)
        qT = sb("qT", [D, TOK], F32)
        kT = sb("kT", [D, TOK], F32)
        sim = sb("sim", [P, NT, N], F32)
        att = sb("att", [P, NT, N], F32)
        work = sb("work", [P, TPB, N], F32)
        top8 = sb("top8", [P, TPB, 8], F32)
        xnT = sb("xnT", [P, TPB, KC, P], F32)
        rw = sb("rw", [P, KC, E], F32)
        gam = sb("gam", [P, 1], F32)
        g_full = sb("g_full", [P, 1], F32)
        g_half = sb("g_half", [P, 1], F32)
        g_rest = sb("g_rest", [P, 1], F32)
        g_neg = sb("g_neg", [P, 1], F32)
        stats = sb("stats", [P, NT, 6], F32)
        mv1 = sb("mv1", [P, NT, 2], F32)
        mv2 = sb("mv2", [P, NT, 2], F32)
        ve = sb("ve", [P, NT], F32)
        rstd = sb("rstd", [P, NT], F32)
        lnb = sb("lnb", [P, NT], F32)
        lna = sb("lna", [P, NT], F32)
        ln_scale = sb("ln_scale", [P, NT], F32)
        ln_bias = sb("ln_bias", [P, NT], F32)
        ve2 = sb("ve2", [P, NT], F32)
        rstd2 = sb("rstd2", [P, NT], F32)
        nm2 = sb("nm2", [P, NT], F32)
        nmr2 = sb("nmr2", [P, NT], F32)
        minus_half = sb("minus_half", [P, NT], F32)
        ident = sb("ident", [P, P], F32)
        ones_f = sb("ones_f", [P, P], F32)
        earlier = sb("earlier", [P, P], F16)
        ones_h = sb("ones_h", [P, P], F16)
        iota_e = sb("iota_e", [P, E], F32)
        iota_lo = sb("iota_lo", [P, P], F32)
        iota_hi = sb("iota_hi", [P, E * MAXT], F32)
        id1 = sb("id1", [P, NT], F32)
        lim = sb("lim", [P, MAXT], F32)
        lmax = sb("lmax", [P, NT, 8], F32)
        lidx = sb("lidx", [P, NT, 8], U32)
        diff = sb("diff", [P, NT], F32)
        prob = sb("prob", [P, 2, NT], F32)
        idxf = sb("idxf", [P, B, 2, TPB], F32)
        onehot = sb("onehot", [P, B, 2, TPB, E], F32)
        picked = sb("picked", [P, NT, E], F16)
        before = sb("before", [P, NT + 1, E], F16)
        wsel = sb("wsel", [P, 2, TPB, E], F32)
        rsel = sb("rsel", [P, 2, TPB, E], F32)
        rank = sb("rank", [P, 2, TPB], F32)
        rank_i = sb("rank_i", [P, 2, TPB], I32)
        lo_i = sb("lo_i", [P, 2, TPB], I32)
        hi_i = sb("hi_i", [P, 2, TPB], I32)
        lo_f = sb("lo_f", [P, 2, TPB], F32)
        hi_f = sb("hi_f", [P, 2, TPB], F32)
        oh_lo = sb("oh_lo", [P, 2, TPB, P], F16)
        oh_hi = sb("oh_hi", [P, 2, TPB, E * MAXT], F16)
        id_hi = sb("id_hi", [P, 2, TPB, E * MAXT], F16)
        idm = sb("idm", [P, E * MAXT], F32)
        pad = sb("pad", [P, E * MAXT], F32)
        gather_ids = sb("gather_ids", [P, E * MAXT + 1], U32)
        scatter_ids = sb("scatter_ids", [P, MAXT + E * MAXT + 1], U32)
        counts = sb("counts", [P, E], F32)
        over = sb("over", [P, E, MAXT - 2], F32)
        extra = sb("extra", [P, E], F32)
        extra_before = sb("extra_before", [P, E], F32)
        control = sb("control", [P, E], F32)
        ctl = sb("ctl", [P, E], I32)
        raw = [sb(f"raw{i}", [P, W_COLS], F32) for i in range(2)]
        w_hi = [sb(f"w_hi{i}", [P, W_COLS], F32R) for i in range(2)]
        w_lo = [sb(f"w_lo{i}", [P, W_COLS], F32R) for i in range(2)]
        silu = [sb(f"silu{c}", [P, FCH], F32) for c in range(2)]
        ht_hi = sb("ht_hi", [P, FB, P], F32R)
        ht_lo = sb("ht_lo", [P, FB, P], F32R)

        A = TileClass("A", sb, sem, 2)
        Bc = TileClass("B", sb, sem, 2)
        C = TileClass("C", sb, sem, 1)

        x_loaded, ctx_loaded, small_loaded = sem("x_loaded"), sem("ctx_loaded"), sem("small_loaded")
        raw_loaded = [sem(f"raw_loaded{i}") for i in range(2)]
        w_hi_ready = [sem(f"w_hi_ready{i}") for i in range(2)]
        w_lo_gu = [sem(f"w_lo_gu{i}") for i in range(2)]
        w_lo_d = [sem(f"w_lo_d{i}") for i in range(2)]
        const_step, const_ready = sem("const_step"), sem("const_ready")
        cleared = sem("cleared")
        waits_passed = sem("waits_passed")
        proj_done, qk_ready = sem("proj_done"), sem("qk_ready")
        sim_done, sim_copied, sig_ready = sem("sim_done"), sem("sim_copied"), sem("sig_ready")
        gamma_ready, gamma_parts = sem("gamma_ready"), sem("gamma_parts")
        stats1_ready, ln1_ready, base_ready = sem("stats1_ready"), sem("ln1_ready"), sem("base_ready")
        pool_step, dve_step = sem("pool_step"), sem("dve_step")
        att_ready, sum_done, x2_ready = sem("att_ready"), sem("sum_done"), sem("x2_ready")
        stats2_ready, ln2_ready, xn_ready = sem("stats2_ready"), sem("ln2_ready"), sem("xn_ready")
        xnt_done, xnt_ready, logits_done = sem("xnt_done"), sem("xnt_ready"), sem("logits_done")
        diff_ready, prob_ready, row_ready = sem("diff_ready"), sem("prob_ready"), sem("row_ready")
        picked_ready, rank_done, ids_in_ready = sem("picked_ready"), sem("rank_done"), sem("ids_in_ready")
        ids_done, counts_done, lists_ready = sem("ids_done"), sem("counts_done"), sem("lists_ready")
        x2_stored, rows_stored = sem("x2_stored"), sem("rows_stored")
        landed = sem("landed")

        block = ctx.enter_context(nc.Block())

        def piece(w, i):
            return w[:, PIECES[i][0]:PIECES[i][0] + PIECES[i][1]]

        def own_instruction(eng):
            eng.sem_inc(waits_passed, 1)

        def load_control(eng, e):
            at = slice(e, e + 1) if isinstance(e, int) else bass.ds(e, 1)
            packed = eng.value_load(ctl[0:1, at], min_val=0, max_val=MAXT * (2 * TOK // P) + MAXT - 2)
            return packed & (MAXT - 1), packed >> LOG_MAXT

        @block.sync
        def _(sp):
            def load_expert(e, slot):
                sp.dma_start(raw[slot][:, 0:KC * F], gate[e]).then_inc(raw_loaded[slot], 16)
                sp.dma_start(raw[slot][:, KC * F:GU_COLS], up[e]).then_inc(raw_loaded[slot], 16)
                sp.dma_start(raw[slot][:, GU_COLS:W_COLS - H], down[e]).then_inc(raw_loaded[slot], 16)
                sp.dma_start(raw[slot][0:FREST, W_COLS - H:W_COLS], down_rest[e]).then_inc(raw_loaded[slot], 16)

            sp.dma_start(ctx_sb[:], ctxT).then_inc(ctx_loaded, 16)
            sp.dma_start(wq_sb[:], wqT).then_inc(ctx_loaded, 16)
            sp.dma_start(wk_sb[:], wkT).then_inc(ctx_loaded, 16)
            sp.dma_start(xs[:], x_view).then_inc(x_loaded, 16)
            sp.dma_start(gam[:], gamma.partition_broadcast(P)).then_inc(small_loaded, 16)
            sp.dma_start(rw[:], routerT).then_inc(small_loaded, 16)
            sp.wait_ge(cleared, 2)
            load_expert(0, 0)
            load_expert(1, 1)
            for t in (A, Bc, C):
                t.start_counts(sp)
            for b in range(B):
                j = slice(b * TPB, (b + 1) * TPB)
                if b < B - 1:
                    sp.wait_ge(x2_ready, b + 1)
                    sp.dma_start(out_view[:, j, :], x2[:, j, :]).then_inc(x2_stored, 16)
                sp.wait_ge(row_ready, b + 1)
                sp.dma_start(scratch_view[:, j, :], xn[:, j, :]).then_inc(rows_stored, 16)
            with sp.Fori(0, E // 2 - 1) as q:
                for s in range(2):
                    sp.wait_ge(w_lo_gu[s], 4 * q + 4)
                    sp.wait_ge(w_lo_d[s], 2 * q + 2)
                    e = 2 * q + s + 2
                    for dst, src in ((raw[s][:, 0:KC * F], gate), (raw[s][:, KC * F:GU_COLS], up),
                                     (raw[s][:, GU_COLS:W_COLS - H], down),
                                     (raw[s][0:FREST, W_COLS - H:W_COLS], down_rest)):
                        sp.dma_start(dst, src[bass.ds(e, 1)].rearrange("a p c -> p (a c)"))\
                          .then_inc(raw_loaded[s], 16)

        @block.tensor
        def _(pe):
            pe.wait_ge(ctx_loaded, 48)
            for w, bank in ((wq_sb, 4), (wk_sb, 6)):
                for half in range(2):
                    nc.tensor.matmul(ps[0:D, bank + half, :], w[:], ctx_sb[:, half * 512:(half + 1) * 512],
                                     start=True, stop=True).then_inc(proj_done, 1)
            pe.wait_ge(qk_ready, 4)
            for b in range(B):
                for r in range(TPB):
                    j = b * TPB + r
                    nc.tensor.matmul(ps[:, SIM[b], r * N:(r + 1) * N], qT[:, j * P:(j + 1) * P],
                                     kT[:, b * N:(b + 1) * N], start=True, stop=True).then_inc(sim_done, 1)
            pe.wait_ge(const_ready, 1)
            pe.wait_ge(small_loaded, 32)
            for b in range(B):
                pe.wait_ge(att_ready, TPB * (b + 1))
                if b:
                    pe.wait_ge(x2_ready, b)
                for r in range(TPB):
                    o = ps[:, SUM, r * N:(r + 1) * N]
                    nc.tensor.matmul(o, ident[:], att[:, b * TPB + r, :], start=True, stop=False)
                    for c in range(TPB):
                        last = nc.tensor.matmul(ps[:, SUM, r * N + c * P:r * N + (c + 1) * P],
                                                att[:, b * TPB + c, r * P:(r + 1) * P], ident[:],
                                                start=False, stop=(c == TPB - 1))
                last.then_inc(sum_done, 1)
                pe.wait_ge(xn_ready, TPB * (b + 1))
                if b:
                    pe.wait_ge(xnt_ready, b)
                for r in range(TPB):
                    for k in range(KC):
                        last = nc.tensor.transpose(ps[:, XNT, (r * KC + k) * P:(r * KC + k + 1) * P],
                                                   xn[:, b * TPB + r, k * P:(k + 1) * P], ident[:])
                last.then_inc(xnt_done, 1)
                pe.wait_ge(xnt_ready, b + 1)
                if b:
                    pe.wait_ge(ids_in_ready, b)
                for r in range(TPB):
                    for k in range(KC):
                        last = nc.tensor.matmul(ps[:, LOG, r * E:(r + 1) * E], xnT[:, r, k, :], rw[:, k, :],
                                                start=(k == 0), stop=(k == KC - 1))
                last.then_inc(logits_done, 1)
                pe.wait_ge(picked_ready, b + 1)
                j = slice(b * TPB, (b + 1) * TPB)
                o = ps[:, LOG, 64:64 + TPB * E]
                nc.tensor.matmul(o, earlier[:], picked[:, j, :].rearrange("p j e -> p (j e)"), start=True, stop=False)
                nc.tensor.matmul(o, ones_h[:], before[:, j, :].rearrange("p j e -> p (j e)"),
                                 start=False, stop=True).then_inc(rank_done, 1)
                if b == B - 1:
                    nc.tensor.matmul(ps[:, LOG, 128:128 + E], ones_h[:], before[:, NT, :],
                                     start=True, stop=True).then_inc(counts_done, 1)
                pe.wait_ge(ids_in_ready, b + 1)
                for c in range(2):
                    for r in range(TPB):
                        last = nc.tensor.matmul(ps[:, IDS, 0:E * MAXT], oh_lo[:, c, r, :], id_hi[:, c, r, :],
                                                start=(b == 0 and c == 0 and r == 0),
                                                stop=(b == B - 1 and c == 1 and r == TPB - 1))
                last.then_inc(ids_done, 1)

            pe.wait_ge(lists_ready, 3)

            def x_transpose(t, n, slot, gathers):
                pe.wait_ge(t.gathered[slot], 16 * gathers)
                for k in range(KC):
                    last = nc.tensor.transpose(ps[:, XB, k * P:(k + 1) * P], t.xg[slot][:, k * P:(k + 1) * P], ident[:])
                last.then_inc(t.x_transposed, 1)

            def gate_up(t, n, c, s):
                if c == 0:
                    pe.wait_ge(t.x_ready, after(n + 1))
                for bank, m in ((GB[c], 0), (UB[c], 1)):
                    for k in range(KC):
                        lo = (m * KC + k) * F + c * FCH
                        hi_w, lo_w = w_hi[s][:, lo:lo + FCH], w_lo[s][:, lo:lo + FCH]
                        o = ps[:, bank, 0:FCH]
                        nc.tensor.matmul(o, t.xt_hi[:, k, :], hi_w, start=(k == 0), stop=False)
                        nc.tensor.matmul(o, t.xt_hi[:, k, :], lo_w, start=False, stop=False)
                        last = nc.tensor.matmul(o, t.xt_lo[:, k, :], hi_w, start=False, stop=(k == KC - 1))
                last.then_inc(t.gu_done[c], 1)

            def h_transpose(t, n):
                for i, blocks in enumerate((range(0, 4), range(4, FB))):
                    pe.wait_ge(t.h_ready[1 - i], after(n + 1))
                    for f in blocks:
                        last = nc.tensor.transpose(ps[:, TB[i], (f % 4) * P:(f % 4 + 1) * P],
                                                   t.h[:, f * P:(f + 1) * P], ident[:])
                    last.then_inc(t.h_transposed[i], 1)

            def down_product(t, n, s):
                o = ps[:, YB, 0:H]
                for f in range(FB):
                    if f == 0:
                        pe.wait_ge(t.ht_ready[0], after(n + 1))
                    if f == 4:
                        pe.wait_ge(t.ht_ready[1], after(n + 1))
                    lo = GU_COLS + f * H
                    hi_w, lo_w = w_hi[s][:, lo:lo + H], w_lo[s][:, lo:lo + H]
                    nc.tensor.matmul(o, ht_hi[:, f, :], hi_w, start=(f == 0), stop=False)
                    nc.tensor.matmul(o, ht_hi[:, f, :], lo_w, start=False, stop=False)
                    last = nc.tensor.matmul(o, ht_lo[:, f, :], hi_w, start=False, stop=(f == FB - 1))
                last.then_inc(t.down_done, 1)

            def expert(q, s, last):
                e = 2 * q + s
                extras, so_far = load_control(pe, e)
                pe.wait_ge(w_lo_gu[s], 4 * q + 4)

                def previous_b_transpose():
                    h_transpose(Bc, e - 1)

                def previous_b_down():
                    pe.wait_ge(A.y_ready, after(e))
                    pe.wait_ge(C.y_ready, after(so_far))
                    down_product(Bc, e - 1, 1 - s)

                pe.wait_ge(A.x_ready, after(e + 1))
                x_transpose(Bc, e, s, q + 1)
                pe.wait_ge(Bc.h_ready[0], after(e))
                gate_up(A, e, 0, s)
                if s == 0:
                    with pe.If(q > 0):
                        previous_b_transpose()
                else:
                    previous_b_transpose()
                pe.wait_ge(Bc.h_ready[1], after(e))
                gate_up(A, e, 1, s)

                def b_down():
                    if s == 0:
                        with pe.If(q > 0):
                            previous_b_down()
                    else:
                        previous_b_down()

                def next_a():
                    if not last:
                        pe.wait_ge(Bc.x_ready, after(e + 1))
                        x_transpose(A, e + 1, 1 - s, q + 1 + s)

                with pe.If(extras > 0):
                    n = so_far
                    pe.wait_ge(Bc.x_ready, after(e + 1))
                    x_transpose(C, n, 0, n + 1)
                    b_down()
                    h_transpose(A, e)
                    gate_up(C, n, 0, s)
                    pe.wait_ge(Bc.y_ready, after(e))
                    pe.wait_ge(w_lo_d[s], 2 * q + 2)
                    down_product(A, e, s)
                    gate_up(C, n, 1, s)
                    next_a()
                    pe.wait_ge(C.h_ready[0], after(n + 1))
                    gate_up(Bc, e, 0, s)
                    h_transpose(C, n)
                    gate_up(Bc, e, 1, s)
                    pe.wait_ge(A.y_ready, after(e + 1))
                    down_product(C, n, s)
                    if not last:
                        pe.wait_ge(A.x_ready, after(e + 2))
                    with pe.If(extras > 1):
                        pe.wait_ge(Bc.h_ready[0], after(e + 1))
                        pe.wait_ge(Bc.h_ready[1], after(e + 1))
                        own_instruction(pe)
                        with pe.Fori(1, extras) as t:
                            n = so_far + t
                            pe.wait_ge(C.y_ready, after(n))
                            x_transpose(C, n, 0, n + 1)
                            gate_up(C, n, 0, s)
                            gate_up(C, n, 1, s)
                            h_transpose(C, n)
                            down_product(C, n, s)
                with pe.Else():
                    b_down()
                    h_transpose(A, e)
                    next_a()
                    gate_up(Bc, e, 0, s)
                    if last:
                        gate_up(Bc, e, 1, s)
                    pe.wait_ge(Bc.y_ready, after(e))
                    pe.wait_ge(w_lo_d[s], 2 * q + 2)
                    down_product(A, e, s)
                    if not last:
                        gate_up(Bc, e, 1, s)

            x_transpose(A, 0, 0, 1)
            with pe.Fori(0, E // 2 - 1) as q:
                expert(q, 0, False)
                expert(q, 1, False)
            expert(E // 2 - 1, 0, False)
            expert(E // 2 - 1, 1, True)
            h_transpose(Bc, E - 1)
            extras, so_far = load_control(pe, E - 1)
            pe.wait_ge(A.y_ready, after(E))
            pe.wait_ge(C.y_ready, after(so_far + extras))
            down_product(Bc, E - 1, 1)

        @block.scalar
        def _(act):
            act.wait_ge(proj_done, 4)
            for half in range(2):
                nc.scalar.activation(qT[:, half * 512:(half + 1) * 512], ps[0:D, 4 + half, :], ACT.Copy,
                                     scale=1.0 / 16.0).then_inc(qk_ready, 1)
                nc.scalar.activation(kT[:, half * 512:(half + 1) * 512], ps[0:D, 6 + half, :], ACT.Copy)\
                  .then_inc(qk_ready, 1)
            for b in range(B):
                j = slice(b * TPB, (b + 1) * TPB)
                act.wait_ge(sim_done, TPB * (b + 1))
                nc.scalar.activation(sim[:, j, :], ps[:, SIM[b], :].rearrange("p (r n) -> p r n", r=TPB),
                                     ACT.Copy).then_inc(sim_copied, 1)
            act.wait_ge(small_loaded, 32)
            nc.scalar.activation(g_full[:], gam[:], ACT.Sigmoid).then_inc(gamma_ready, 1)
            for b in range(B):
                j = slice(b * TPB, (b + 1) * TPB)
                nc.scalar.activation(att[:, j, :], ps[:, SIM[b], :].rearrange("p (r n) -> p r n", r=TPB),
                                     ACT.Sigmoid).then_inc(sig_ready, 1)
            act.wait_ge(ln1_ready, 2)
            for j in range(NT):
                nc.scalar.activation(xs[:, j, :], xs[:, j, :], ACT.Identity, scale=ln_scale[:, j:j + 1],
                                     bias=ln_bias[:, j:j + 1]).then_inc(base_ready, 1)
            act.wait_ge(raw_loaded[0], 64)
            for i in range(len(PIECES)):
                nc.scalar.activation(piece(w_hi[0], i), piece(raw[0], i), ACT.Copy).then_inc(w_hi_ready[0], 1)
            for b in range(B):
                act.wait_ge(ln2_ready, b + 1)
                for r in range(TPB):
                    j = b * TPB + r
                    nc.scalar.activation(xn[:, j, 0:H], x2[:, j, :], ACT.Identity, scale=rstd2[:, j:j + 1],
                                         bias=nmr2[:, j:j + 1]).then_inc(xn_ready, 1)
                act.wait_ge(xnt_done, b + 1)
                if b:
                    act.wait_ge(logits_done, b)
                nc.scalar.activation(xnT[:], ps[:, XNT, :].rearrange("p (r k t) -> p r k t", r=TPB, k=KC), ACT.Copy)\
                  .then_inc(xnt_ready, 1)
                act.wait_ge(diff_ready, b + 1)
                js = slice(b * TPB, (b + 1) * TPB)
                nc.scalar.activation(prob[:, 0, js], diff[:, js], ACT.Sigmoid).then_inc(prob_ready, 1)
                nc.scalar.activation(prob[:, 1, js], diff[:, js], ACT.Sigmoid, scale=-1.0).then_inc(prob_ready, 1)

            def x_hi(t, n):
                act.wait_ge(t.x_transposed, after(n + 1))
                nc.scalar.copy(t.xt_hi[:], ps[:, XB, 0:H].rearrange("p (k t) -> p k t", k=KC))\
                  .then_inc(t.x_hi_ready, 1)

            def gate_silu(t, n, c):
                act.wait_ge(t.gu_done[c], after(n + 1))
                nc.scalar.activation(silu[c][:], ps[:, GB[c], 0:FCH], ACT.Silu).then_inc(t.silu_ready[c], 1)

            def ht_high(t, n):
                for i, (f0, f1) in enumerate(((0, 4), (4, FB))):
                    act.wait_ge(t.h_transposed[i], after(n + 1))
                    nc.scalar.copy(ht_hi[:, f0:f1, :],
                                   ps[:, TB[i], 0:(f1 - f0) * P].rearrange("p (f t) -> p f t", t=P)).then_inc(t.ht_hi_ready[i], 1)

            def expert(q, s, last):
                e = 2 * q + s
                extras, so_far = load_control(act, e)

                def split_next(*pieces):
                    if last:
                        return
                    for i in pieces:
                        if i == 0:
                            act.wait_ge(raw_loaded[1 - s], 64 * (q + s + 1))
                            act.wait_ge(Bc.gu_done[1], after(e))
                            act.wait_ge(C.gu_done[1], after(so_far))
                        if i == len(GU_PIECES):
                            act.wait_ge(Bc.down_done, after(e))
                            act.wait_ge(C.down_done, after(so_far))
                        nc.scalar.copy(piece(w_hi[1 - s], i), piece(raw[1 - s], i))\
                          .then_inc(w_hi_ready[1 - s], 1)

                x_hi(Bc, e)
                gate_silu(A, e, 0)
                split_next(0)
                if s == 0:
                    with act.If(q > 0):
                        ht_high(Bc, e - 1)
                else:
                    ht_high(Bc, e - 1)
                split_next(1)
                gate_silu(A, e, 1)
                with act.If(extras > 0):
                    n = so_far
                    x_hi(C, n)
                    ht_high(A, e)
                    gate_silu(C, n, 0)
                    split_next(2)
                    gate_silu(C, n, 1)
                    if not last:
                        x_hi(A, e + 1)
                    split_next(3)
                    gate_silu(Bc, e, 0)
                    ht_high(C, n)
                with act.Else():
                    ht_high(A, e)
                    if not last:
                        x_hi(A, e + 1)
                    split_next(2)
                    gate_silu(Bc, e, 0)
                    split_next(3)
                split_next(4)
                gate_silu(Bc, e, 1)
                split_next(5)
                with act.If(extras > 1):
                    with act.Fori(1, extras) as t:
                        n = so_far + t
                        x_hi(C, n)
                        gate_silu(C, n, 0)
                        gate_silu(C, n, 1)
                        ht_high(C, n)

            nc.scalar.preload_act_table(ACT.Silu)
            act.wait_ge(lists_ready, 3)
            x_hi(A, 0)
            with act.Fori(0, E // 2 - 1) as q:
                expert(q, 0, False)
                expert(q, 1, False)
            expert(E // 2 - 1, 0, False)
            expert(E // 2 - 1, 1, True)
            ht_high(Bc, E - 1)

        @block.vector
        def _(dve):
            steps = [0]

            def step(ins):
                steps[0] += 1
                ins.then_inc(dve_step, 1)
                dve.wait_ge(dve_step, steps[0])

            for s in range(2):
                nc.vector.memset(raw[s][:, W_COLS - H:W_COLS], 0.0).then_inc(cleared, 1)
            for t in (A, Bc, C):
                nc.vector.memset(t.h[:, F:FB * P], 0.0).then_inc(cleared, 1)
            step(nc.vector.memset(before[:, 0, :], 0.0))
            dve.wait_ge(x_loaded, 16)
            for j in range(NT):
                step(nc.vector.bn_stats(stats[:, j, :], xs[:, j, :]))
                nc.vector.bn_aggr(mv1[:, j, :], stats[:, j, :]).then_inc(stats1_ready, 1)

            def topk(b, between):
                dve.wait_ge(sim_copied, b + 1)
                if b:
                    dve.wait_ge(att_ready, TPB * b)
                done = [steps[0]] * TPB
                for i in range(ROUNDS):
                    for r in range(TPB):
                        dve.wait_ge(dve_step, done[r])
                        nc.vector.max(top8[:, r, :], sim[:, b * TPB + r, :] if i == 0 else work[:, r, :])\
                          .then_inc(dve_step, 1)
                        steps[0] += 1
                        done[r] = steps[0]
                    if i < ROUNDS - 1:
                        for r in range(TPB):
                            dve.wait_ge(dve_step, done[r])
                            nc.vector.match_replace(work[:, r, :], top8[:, r, :],
                                                    sim[:, b * TPB + r, :] if i == 0 else work[:, r, :], LOWEST)\
                              .then_inc(dve_step, 1)
                            steps[0] += 1
                            done[r] = steps[0]
                    between(i)
                dve.wait_ge(dve_step, max(done))
                dve.wait_ge(sig_ready, b + 1)
                last_kept = (KTOP - 1) % 8
                for r in range(TPB):
                    j = b * TPB + r
                    nc.vector.scalar_tensor_tensor(att[:, j, :], sim[:, j, :], top8[:, r, last_kept:last_kept + 1],
                                                   att[:, j, :], ALU.is_ge, ALU.mult).then_inc(att_ready, 1)

            def residual(b):
                j = slice(b * TPB, (b + 1) * TPB)
                dve.wait_ge(sum_done, b + 1)
                dve.wait_ge(base_ready, TPB * (b + 1))
                dve.wait_ge(gamma_parts, 3)
                nc.vector.scalar_tensor_tensor(x2[:, j, :], ps[:, SUM, :].rearrange("p (r n) -> p r n", r=TPB),
                                               g_half[:, 0:1], xs[:, j, :], ALU.mult, ALU.add).then_inc(x2_ready, 1)
                dve.wait_ge(x2_ready, b + 1)
                for r in range(TPB):
                    nc.vector.bn_stats(stats[:, b * TPB + r, :], x2[:, b * TPB + r, :]).then_inc(dve_step, 1)
                steps[0] += TPB
                dve.wait_ge(dve_step, steps[0])
                for r in range(TPB):
                    nc.vector.bn_aggr(mv2[:, b * TPB + r, :], stats[:, b * TPB + r, :]).then_inc(stats2_ready, 1)

            def pick(b):
                dve.wait_ge(logits_done, b + 1)
                for r in range(TPB):
                    nc.vector.max(lmax[:, b * TPB + r, :], ps[:, LOG, r * E:(r + 1) * E]).then_inc(dve_step, 1)
                steps[0] += TPB
                dve.wait_ge(dve_step, steps[0])
                j = slice(b * TPB, (b + 1) * TPB)
                nc.vector.tensor_tensor(diff[:, j], lmax[:, j, 0], lmax[:, j, 1], ALU.subtract).then_inc(diff_ready, 1)
                for r in range(TPB):
                    nc.vector.max_index(lidx[:, b * TPB + r, :], lmax[:, b * TPB + r, :],
                                        ps[:, LOG, r * E:(r + 1) * E]).then_inc(dve_step, 1)
                steps[0] += TPB
                dve.wait_ge(dve_step, steps[0])
                step(nc.vector.tensor_copy(idxf[:, b], lidx[:, j, 0:2].rearrange("p j c -> p c j")))
                dve.wait_ge(const_ready, 1)
                bc = [P, 2, TPB, E]
                step(nc.vector.tensor_tensor(onehot[:, b], iota_e[:, None, None, :].to_broadcast(bc),
                                             idxf[:, b, :, :, None].to_broadcast(bc), ALU.is_equal))
                step(nc.vector.tensor_tensor(picked[:, j, :], onehot[:, b, 0], onehot[:, b, 1], ALU.add))
                for r in range(TPB):
                    t = b * TPB + r
                    ins = nc.vector.tensor_tensor(before[:, t + 1, :], before[:, t, :], picked[:, t, :], ALU.add)
                    if r < TPB - 1:
                        step(ins)
                    else:
                        ins.then_inc(picked_ready, 1)
                dve.wait_ge(picked_ready, b + 1)
                dve.wait_ge(prob_ready, 2 * (b + 1))
                step(nc.vector.tensor_tensor(wsel[:], onehot[:, b], prob[:, :, j][:, :, :, None].to_broadcast(bc),
                                             ALU.mult))
                nc.vector.tensor_tensor(xn[:, j, H:ROW], wsel[:, 0], wsel[:, 1], ALU.add).then_inc(row_ready, 1)

            def place(b):
                dve.wait_ge(rank_done, b + 1)
                if b:
                    dve.wait_ge(ids_done, b)
                bc = [P, 2, TPB, E]
                step(nc.vector.tensor_tensor(
                    rsel[:], onehot[:, b],
                    ps[:, LOG, 64:64 + TPB * E].rearrange("p (r e) -> p r e", e=E)[:, None].to_broadcast(bc), ALU.mult))
                step(nc.vector.tensor_reduce(rank[:], rsel[:], AX.X, ALU.add))
                step(nc.vector.tensor_copy(rank_i[:], rank[:]))
                nc.vector.tensor_single_scalar(lo_i[:], rank_i[:], P - 1, ALU.bitwise_and).then_inc(dve_step, 1)
                nc.vector.tensor_single_scalar(hi_i[:], rank_i[:], 7, ALU.arith_shift_right).then_inc(dve_step, 1)
                steps[0] += 2
                dve.wait_ge(dve_step, steps[0])
                nc.vector.tensor_copy(lo_f[:], lo_i[:]).then_inc(dve_step, 1)
                nc.vector.scalar_tensor_tensor(hi_f[:], idxf[:, b], float(MAXT), hi_i[:], ALU.mult, ALU.add)\
                  .then_inc(dve_step, 1)
                steps[0] += 2
                dve.wait_ge(dve_step, steps[0])
                bl, bh = [P, 2, TPB, P], [P, 2, TPB, E * MAXT]
                step(nc.vector.tensor_tensor(oh_hi[:], iota_hi[:, None, None, :].to_broadcast(bh),
                                             hi_f[:, :, :, None].to_broadcast(bh), ALU.is_equal))
                step(nc.vector.tensor_tensor(oh_lo[:], iota_lo[:, None, None, :].to_broadcast(bl),
                                             lo_f[:, :, :, None].to_broadcast(bl), ALU.is_equal))
                nc.vector.tensor_tensor(id_hi[:], oh_hi[:],
                                        id1[:, None, b * TPB:(b + 1) * TPB, None].to_broadcast(bh),
                                        ALU.mult).then_inc(ids_in_ready, 1)

            for b in range(B):
                def between(i, b=b):
                    if b and i == 1:
                        residual(b - 1)
                    if b and i == 5:
                        pick(b - 1)
                    if b and i == 8:
                        place(b - 1)
                topk(b, between)
            residual(B - 1)
            pick(B - 1)
            dve.wait_ge(counts_done, 1)
            step(nc.vector.tensor_copy(counts[:], ps[:, LOG, 128:128 + E]))
            bc = [P, E, MAXT - 2]
            step(nc.vector.tensor_tensor(over[:], counts[:, :, None].to_broadcast(bc),
                                         lim[:, None, 2:MAXT].to_broadcast(bc), ALU.is_gt))
            step(nc.vector.tensor_reduce(extra[:], over[:], AX.X, ALU.add))
            step(nc.vector.memset(extra_before[:, 0:1], 0.0))
            for e in range(1, E):
                step(nc.vector.tensor_tensor(extra_before[:, e:e + 1], extra_before[:, e - 1:e], extra[:, e - 1:e],
                                             ALU.add))
            step(nc.vector.scalar_tensor_tensor(control[:], extra_before[:], float(MAXT), extra[:], ALU.mult, ALU.add))
            nc.vector.tensor_copy(ctl[:], control[:]).then_inc(lists_ready, 1)
            place(B - 1)
            dve.wait_ge(ids_done, B)
            nc.vector.tensor_scalar(idm[:], ps[:, IDS, 0:E * MAXT], -1.0, 0.0, ALU.add, ALU.max).then_inc(dve_step, 1)
            nc.vector.tensor_scalar(pad[:], ps[:, IDS, 0:E * MAXT], 0.0, SKIP, ALU.is_equal, ALU.mult)\
              .then_inc(dve_step, 1)
            steps[0] += 2
            dve.wait_ge(dve_step, steps[0])
            nc.vector.tensor_copy(gather_ids[:, 0:E * MAXT], idm[:]).then_inc(lists_ready, 1)
            nc.vector.tensor_tensor(scatter_ids[:, MAXT:MAXT + E * MAXT], idm[:], pad[:], ALU.add).then_inc(lists_ready, 1)
            dve.wait_ge(lists_ready, 3)

            def x_lo(t, n, slot, e):
                dve.wait_ge(t.x_hi_ready, after(n + 1))
                nc.vector.tensor_copy(t.weight[slot][:], t.xg[slot][:, bass.ds(H + e, 1)]).then_inc(t.weight_ready, 1)
                nc.vector.tensor_tensor(t.xt_lo[:], ps[:, XB, 0:H].rearrange("p (k t) -> p k t", k=KC),
                                        t.xt_hi[:].bitcast(F32), ALU.subtract).then_inc(t.x_ready, 1)

            def hidden(t, n, c):
                dve.wait_ge(t.silu_ready[c], after(n + 1))
                dve.wait_ge(t.h_transposed[1], after(n))
                nc.vector.tensor_tensor(t.h[:, c * FCH:(c + 1) * FCH], silu[c][:], ps[:, UB[c], 0:FCH],
                                        ALU.mult).then_inc(t.h_ready[c], 1)

            def ht_low(t, n):
                for i, (f0, f1) in enumerate(((0, 4), (4, FB))):
                    dve.wait_ge(t.ht_hi_ready[i], after(n + 1))
                    nc.vector.tensor_tensor(ht_lo[:, f0:f1, :],
                                            ps[:, TB[i], 0:(f1 - f0) * P].rearrange("p (f t) -> p f t", t=P),
                                            ht_hi[:, f0:f1, :].bitcast(F32), ALU.subtract).then_inc(t.ht_ready[i], 1)

            def weigh(t, n, slot, later, listed):
                dve.wait_ge(t.down_done, after(n + 1))
                dve.wait_ge(later.to_listed, after(listed))
                nc.vector.tensor_scalar(t.y[:], ps[:, YB, 0:H], t.weight[slot][:, 0:1], None,
                                        ALU.mult).then_inc(t.y_ready, 1)

            def expert(q, s, last):
                e = 2 * q + s
                extras, so_far = load_control(dve, e)

                def split_next(*pieces):
                    if last:
                        return
                    for i in pieces:
                        dve.wait_ge(w_hi_ready[1 - s], len(PIECES) * (q + s) + i + 1)
                        nc.vector.tensor_tensor(piece(w_lo[1 - s], i), piece(raw[1 - s], i),
                                                piece(w_hi[1 - s], i).bitcast(F32), ALU.subtract)\
                          .then_inc((w_lo_gu if i < len(GU_PIECES) else w_lo_d)[1 - s], 1)

                x_lo(Bc, e, s, e)
                hidden(A, e, 0)
                if s == 0:
                    with dve.If(q > 0):
                        ht_low(Bc, e - 1)
                else:
                    ht_low(Bc, e - 1)
                split_next(1)
                hidden(A, e, 1)

                def weigh_b():
                    if s == 0:
                        with dve.If(q > 0):
                            weigh(Bc, e - 1, 1 - s, A, e)
                    else:
                        weigh(Bc, e - 1, 1 - s, A, e)

                with dve.If(extras > 0):
                    n = so_far
                    x_lo(C, n, 0, e)
                    weigh_b()
                    ht_low(A, e)
                    hidden(C, n, 0)
                    weigh(A, e, s, Bc, e)
                    split_next(2)
                    hidden(C, n, 1)
                    if not last:
                        x_lo(A, e + 1, 1 - s, e + 1)
                    hidden(Bc, e, 0)
                    ht_low(C, n)
                    split_next(3)
                    hidden(Bc, e, 1)
                    weigh(C, n, 0, Bc, e)
                with dve.Else():
                    weigh_b()
                    ht_low(A, e)
                    if not last:
                        x_lo(A, e + 1, 1 - s, e + 1)
                    split_next(2)
                    hidden(Bc, e, 0)
                    split_next(3)
                    if last:
                        hidden(Bc, e, 1)
                    weigh(A, e, s, Bc, e)
                    if not last:
                        hidden(Bc, e, 1)
                split_next(5)
                with dve.If(extras > 1):
                    with dve.Fori(1, extras) as t:
                        n = so_far + t
                        x_lo(C, n, 0, e)
                        hidden(C, n, 0)
                        hidden(C, n, 1)
                        ht_low(C, n)
                        weigh(C, n, 0, C, n + 1)

            x_lo(A, 0, 0, 0)
            with dve.Fori(0, E // 2 - 1) as q:
                expert(q, 0, False)
                expert(q, 1, False)
            expert(E // 2 - 1, 0, False)
            expert(E // 2 - 1, 1, True)
            ht_low(Bc, E - 1)
            weigh(Bc, E - 1, 1, A, E)

        @block.gpsimd
        def _(pool):
            steps = [0]

            def step(ins):
                steps[0] += 1
                ins.then_inc(pool_step, 1)
                pool.wait_ge(pool_step, steps[0])

            nc.gpsimd.memset(ones_f[:], 1.0).then_inc(const_step, 1)
            nc.gpsimd.memset(ones_h[:], 1.0).then_inc(const_step, 1)
            nc.gpsimd.memset(minus_half[:], -0.5).then_inc(const_step, 1)
            pool.wait_ge(const_step, 3)
            nc.gpsimd.affine_select(out=ident[:], in_=ones_f[:], compare_op=ALU.is_equal, fill=0.0, base=0,
                                    pattern=[[-1, P]], channel_multiplier=1).then_inc(const_step, 1)
            nc.gpsimd.affine_select(out=earlier[:], in_=ones_h[:], compare_op=ALU.is_gt, fill=0.0, base=0,
                                    pattern=[[1, P]], channel_multiplier=-1).then_inc(const_step, 1)
            imprecise = dict(allow_small_or_imprecise_dtypes=True)
            nc.gpsimd.iota(iota_e[:], pattern=[[1, E]], base=0, channel_multiplier=0, **imprecise).then_inc(const_step, 1)
            nc.gpsimd.iota(iota_lo[:], pattern=[[1, P]], base=0, channel_multiplier=0, **imprecise).then_inc(const_step, 1)
            nc.gpsimd.iota(iota_hi[:], pattern=[[1, E * MAXT]], base=0, channel_multiplier=0, **imprecise)\
              .then_inc(const_step, 1)
            nc.gpsimd.iota(id1[:], pattern=[[P, NT]], base=1, channel_multiplier=1, **imprecise).then_inc(const_step, 1)
            nc.gpsimd.iota(lim[:], pattern=[[P, MAXT]], base=0, channel_multiplier=0, **imprecise).then_inc(const_step, 1)
            pool.wait_ge(const_step, 10)
            pool.sem_inc(const_ready, 1)
            pool.wait_ge(gamma_ready, 1)
            nc.gpsimd.tensor_scalar(g_half[:], g_full[:], 0.5, 0.0, ALU.mult, ALU.add).then_inc(gamma_parts, 1)
            nc.gpsimd.tensor_scalar(g_rest[:], g_full[:], -1.0, 1.0, ALU.mult, ALU.add).then_inc(gamma_parts, 1)
            nc.gpsimd.tensor_scalar(g_neg[:], g_full[:], 1.0, -1.0, ALU.mult, ALU.add).then_inc(gamma_parts, 1)
            pool.wait_ge(stats1_ready, NT)
            pool.wait_ge(gamma_parts, 3)
            step(nc.gpsimd.tensor_scalar(ve[:], mv1[:, :, 1], 1.0, EPS, ALU.mult, ALU.add))
            step(nc.gpsimd.tensor_tensor(rstd[:], ve[:], minus_half[:], ALU.pow))
            nc.gpsimd.tensor_scalar(ln_scale[:], rstd[:], g_rest[:, 0:1], 1.0, ALU.mult, ALU.add).then_inc(ln1_ready, 1)
            step(nc.gpsimd.tensor_tensor(lnb[:], rstd[:], mv1[:, :, 0], ALU.mult))
            nc.gpsimd.tensor_scalar(ln_bias[:], lnb[:], g_neg[:, 0:1], 0.0, ALU.mult, ALU.add).then_inc(ln1_ready, 1)

            def split_lo(slot, uses, i):
                pool.wait_ge(w_hi_ready[slot], len(PIECES) * uses + i + 1)
                nc.gpsimd.tensor_tensor(piece(w_lo[slot], i), piece(raw[slot], i), piece(w_hi[slot], i).bitcast(F32),
                                        ALU.subtract).then_inc((w_lo_gu if i < len(GU_PIECES) else w_lo_d)[slot], 1)

            for b in range(B):
                j = slice(b * TPB, (b + 1) * TPB)
                pool.wait_ge(stats2_ready, TPB * (b + 1))
                step(nc.gpsimd.tensor_scalar(ve2[:, j], mv2[:, j, 1], 1.0, EPS, ALU.mult, ALU.add))
                step(nc.gpsimd.tensor_tensor(rstd2[:, j], ve2[:, j], minus_half[:, j], ALU.pow))
                step(nc.gpsimd.tensor_tensor(nm2[:, j], rstd2[:, j], mv2[:, j, 0], ALU.mult))
                nc.gpsimd.tensor_scalar(nmr2[:, j], nm2[:, j], -1.0, 0.0, ALU.mult, ALU.add).then_inc(ln2_ready, 1)
                if b == B - 1:
                    pool.dma_start(out_view[:, j, :], x2[:, j, :]).then_inc(landed, 16)
                if b < B - 1:
                    split_lo(0, 0, 2 * b)
                    split_lo(0, 0, 2 * b + 1)

            def gather(t, n, e, tile, slot):
                own_instruction(pool)
                nc.gpsimd.tensor_copy(t.from_rows[slot][:], gather_ids[:, bass.ds(e * MAXT + tile, 1)])\
                  .then_inc(t.from_listed, 1)
                pool.wait_ge(t.from_listed, after(n + 1))
                own_instruction(pool)
                pool.indirect_dma_start(out=t.xg[slot][:], out_offset=None, in_=scratch,
                                        in_offset=bass.IndirectOffsetOnAxis(ap=t.from_rows[slot][:], axis=0))\
                    .then_inc(t.gathered[slot], 16)

            def scatter(t, n, e, tile, scatters_before):
                pool.wait_ge(landed, 16 * (scatters_before + 1))
                own_instruction(pool)
                nc.gpsimd.tensor_copy(t.to_rows[:], scatter_ids[:, bass.ds((e + 1) * MAXT + tile, 1)])\
                  .then_inc(t.to_listed, 1)
                pool.wait_ge(t.to_listed, after(n + 1))
                pool.wait_ge(t.y_ready, after(n + 1))
                own_instruction(pool)
                pool.indirect_dma_start(out=out_rows, in_=t.y[:], in_offset=None,
                                        out_offset=bass.IndirectOffsetOnAxis(ap=t.to_rows[:], axis=0),
                                        bounds_check=TOK - 1, oob_is_err=False, compute_op=ALU.add)\
                    .then_inc(landed, 16)

            pool.wait_ge(lists_ready, 3)
            pool.wait_ge(rows_stored, 16 * B)
            gather(A, 0, 0, 0, 0)
            gather(Bc, 0, 0, 1, 0)
            first_extras, _ = load_control(pool, 0)
            with pool.If(first_extras > 0):
                gather(C, 0, 0, 2, 0)
            pool.wait_ge(x2_stored, 16 * (B - 1))
            pool.wait_ge(landed, 16)

            def expert(q, s, last):
                e = 2 * q + s
                extras, so_far = load_control(pool, e)
                if not last:
                    next_extras, next_so_far = load_control(pool, e + 1)
                    gather(A, e + 1, e + 1, 0, 1 - s)
                    pool.wait_ge(Bc.weight_ready, after(e))
                    gather(Bc, e + 1, e + 1, 1, 1 - s)

                def previous_b():
                    split_lo(s, q, 4)
                    scatter(Bc, e - 1, e - 1, 1, 2 * e - 1 + so_far)

                if s == 0:
                    with pool.If(q > 0):
                        previous_b()
                else:
                    previous_b()

                def next_c():
                    with pool.If(next_extras > 0):
                        pool.wait_ge(C.weight_ready, after(next_so_far))
                        gather(C, next_so_far, e + 1, 2, 0)

                if not last:
                    split_lo(1 - s, q + s, 0)
                    with pool.If(extras < 2):
                        next_c()
                scatter(A, e, e, 0, 2 * e + so_far)
                with pool.If(extras > 0):
                    scatter(C, so_far, e, 2, 2 * e + 1 + so_far)
                with pool.If(extras > 1):
                    with pool.Fori(1, extras) as t:
                        n = so_far + t
                        pool.wait_ge(C.weight_ready, after(n))
                        gather(C, n, e, 2 + t, 0)
                        scatter(C, n, e, 2 + t, 2 * e + 1 + n)
                    if not last:
                        next_c()

            with pool.Fori(0, E // 2 - 1) as q:
                expert(q, 0, False)
                expert(q, 1, False)
            expert(E // 2 - 1, 0, False)
            expert(E // 2 - 1, 1, True)
            extras, so_far = load_control(pool, E - 1)
            scatter(Bc, E - 1, E - 1, 1, 2 * E - 1 + so_far + extras)
            pool.wait_ge(landed, 16 * (2 * E + so_far + extras + 1))
            own_instruction(pool)


def kernel(**inputs):
    import numpy as np
    import concourse.bacc as bacc
    from concourse import mybir as my
    from concourse.bass_utils import run_bass_kernel_spmd as run

    a = {k: np.asarray(v) for k, v in inputs.items()}
    e, f, h = a["L0_ffn_gate_w"].shape
    kc = h // 128
    whole = f // 128 * 128
    down_t = a["L0_ffn_down_w"].transpose(0, 2, 1)

    def contraction_first(w):
        return w.reshape(e, f, kc, 128).transpose(0, 3, 2, 1).reshape(e, 128, kc * f)

    laid_out = {
        "x": a["x"],
        "ctxT": a["ctx_512"].reshape(-1, a["ctx_512"].shape[-1]).T,
        "wqT": a["L0_xattn_Wq"].T,
        "wkT": a["L0_xattn_Wk"].T,
        "gamma": a["L0_xattn_gamma_raw"].reshape(1),
        "routerT": a["L0_ffn_router_w"].reshape(e, kc, 128).transpose(2, 1, 0),
        "gate": contraction_first(a["L0_ffn_gate_w"]),
        "up": contraction_first(a["L0_ffn_up_w"]),
        "down": down_t[:, :whole].reshape(e, whole // 128, 128, h).transpose(0, 2, 1, 3).reshape(e, 128, -1),
        "down_rest": down_t[:, whole:],
    }
    nc = bacc.Bacc("TRN2", target_bir_lowering=False, num_devices=1)
    arrays, args = {}, []
    for name, v in laid_out.items():
        v = np.ascontiguousarray(v)
        arrays[f"in_{name}"] = v
        args.append(nc.dram_tensor(f"in_{name}", v.shape, my.dt.from_np(v.dtype), kind="ExternalInput").ap())
    args.append(nc.dram_tensor("out_0", a["x"].shape, my.dt.from_np(a["x"].dtype), kind="ExternalOutput").ap())
    xattn_moe_kernel(nc, *args)
    return run(nc, [arrays], core_ids=[0]).results[0]["out_0"]
```

```python
import concourse.bass as bass
from concourse import mybir
from contextlib import ExitStack

F32 = mybir.dt.float32
F32R = mybir.dt.float32r
F16 = mybir.dt.float16
I32 = mybir.dt.int32
U32 = mybir.dt.uint32
ALU = mybir.AluOpType
ACT = mybir.ActivationFunctionType
AX = mybir.AxisListType

P = 128
B, N, D = 4, 256, 64
H = 256
TOK = B * N
NT = TOK // P
TPB = N // P
BPG = 2
NG = B // BPG
TPG = BPG * TPB
KTOP = int(N * 0.3)
ROUNDS = (KTOP + 7) // 8
E, F = 8, 688
KC = H // P
FCH = F // 2
FB = (F + P - 1) // P
FREST = F - (FB - 1) * P
GU_COLS = 2 * KC * F
W_COLS = GU_COLS + FB * H
MAXT = TOK // P
LOG_MAXT = MAXT.bit_length() - 1
EPS = 1e-5
LOWEST = -3.4e38
STEPS_OF_GUESS = 3
GUESS_DENSITY = 130.0
WINDOW = 16
COUNT_MID = KTOP - (WINDOW + 1) / 2
TARGET = KTOP - WINDOW // 2
SKIP = 4096.0
ROW = H + E

GU_PIECES = [(i * F, F) for i in range(2 * KC)]
D_PIECES = [(GU_COLS + i * (FB * H // 2), FB * H // 2) for i in range(2)]
PIECES = GU_PIECES + D_PIECES

SIM = [0, 1, 2, 3]
PROJ = [4, 5, 6, 7]
XNT, LOG, IDS = [4, 5], 6, 7
GB, UB = [0, 2], [1, 3]
TB = [4, 6]
XB, YB = 5, 7


def after(tiles):
    return tiles + 1


class TileClass:

    def __init__(self, name, sb, sem, gather_slots):
        self.name = name
        self.xg = [sb(f"xg{name}{i}", [P, ROW], F32) for i in range(gather_slots)]
        self.xt_hi = sb(f"xt_hi{name}", [P, KC, P], F32R)
        self.xt_lo = sb(f"xt_lo{name}", [P, KC, P], F32R)
        self.h = sb(f"h{name}", [P, FB * P], F32)
        self.y = sb(f"y{name}", [P, H], F32)
        self.weight = [sb(f"weight{name}{i}", [P, 1], F32) for i in range(gather_slots)]
        self.from_rows = [sb(f"from_rows{name}{i}", [P, 1], U32) for i in range(gather_slots)]
        self.to_rows = sb(f"to_rows{name}", [P, 1], U32)
        self.gathered = [sem(f"gathered{name}{i}") for i in range(gather_slots)]
        self.from_listed = sem(f"from_listed{name}")
        self.to_listed = sem(f"to_listed{name}")
        self.x_transposed = sem(f"x_transposed{name}")
        self.x_hi_ready = sem(f"x_hi_ready{name}")
        self.x_ready = sem(f"x_ready{name}")
        self.weight_ready = sem(f"weight_ready{name}")
        self.gu_done = [sem(f"gu_done{name}{c}") for c in range(2)]
        self.silu_ready = [sem(f"silu_ready{name}{c}") for c in range(2)]
        self.h_ready = [sem(f"h_ready{name}{c}") for c in range(2)]
        self.h_transposed = [sem(f"h_transposed{name}{c}") for c in range(2)]
        self.ht_hi_ready = [sem(f"ht_hi_ready{name}{c}") for c in range(2)]
        self.ht_ready = [sem(f"ht_ready{name}{c}") for c in range(2)]
        self.down_done = sem(f"down_done{name}")
        self.y_ready = sem(f"y_ready{name}")

    def start_counts(self, eng):
        for s in (self.from_listed, self.to_listed, self.x_transposed, self.x_hi_ready, self.x_ready, self.weight_ready,
                  *self.gu_done,
                  *self.silu_ready, *self.h_ready, *self.h_transposed, *self.ht_hi_ready, *self.ht_ready,
                  self.down_done, self.y_ready):
            eng.sem_inc(s, 1)


def xattn_moe_kernel(nc, x, ctxT, wq, wk, gamma, routerT, gate, up, down, down_rest, out):
    scratch = nc.dram_tensor("xn_rows", (TOK, ROW), F32, kind="Internal").ap()
    x_view = x.rearrange("b (r p) d -> p (b r) d", p=P)
    out_view = out.rearrange("b (r p) d -> p (b r) d", p=P)
    out_rows = out.rearrange("b n d -> (b n) d")
    scratch_view = scratch.rearrange("(j p) d -> p j d", p=P)

    ctx = ExitStack()
    with ctx:
        def sb(name, shape, dt):
            return ctx.enter_context(nc.sbuf_tensor(name, shape, dt))

        def sem(name):
            return ctx.enter_context(nc.semaphore(name))

        ps = ctx.enter_context(nc.psum_tensor("ps", [P, 8, 512], F32))

        xs = sb("xs", [P, NT, H], F32)
        x2 = sb("x2", [P, NT, H], F32)
        xn = sb("xn", [P, NT, ROW], F32)
        ctx_sb = sb("ctx_sb", [D, TOK], F32)
        wq_sb = sb("wq_sb", [D, D], F32)
        wk_sb = sb("wk_sb", [D, D], F32)
        m_sb = sb("m_sb", [D, D], F32)
        mT = sb("mT", [D, TOK], F32)
        sim = sb("sim", [P, NT, N], F32)
        att = sb("att", [P, NT, N], F32)
        work = sb("work", [P, TPB, N], F32)
        top = sb("top", [P, NT, WINDOW], F32)
        mvs = sb("mvs", [P, NT, 2], F32)
        deviation = sb("deviation", [P, NT], F32)
        guess = sb("guess", [P, NT], F32)
        guess_base = sb("guess_base", [P, NT], F32)
        slope = sb("slope", [P, NT], F32)
        slope_base = sb("slope_base", [P, NT], F32)
        half = sb("half", [P, NT], F32)
        signs = sb("signs", [P, NT], F32)
        above = sb("above", [P, NT], F32)
        wanted = sb("wanted", [P, NT], F32)
        chosen = sb("chosen", [P, NT, WINDOW], F32)
        threshold = sb("threshold", [P, NT], F32)
        off = sb("off", [P, NT], F32)
        off_squared = sb("off_squared", [P, NT], F32)
        missed = sb("missed", [P, NT], F32)
        missed_sum = sb("missed_sum", [P, 1], F32)
        missed_any = sb("missed_any", [P, 1], I32)
        work1 = sb("work1", [P, N], F32)
        top1 = sb("top1", [P, 8], F32)
        xnT = sb("xnT", [P, TPG, KC, P], F32)
        rw = sb("rw", [P, KC, E], F32)
        gam = sb("gam", [P, 1], F32)
        g_full = sb("g_full", [P, 1], F32)
        g_half = sb("g_half", [P, 1], F32)
        g_rest = sb("g_rest", [P, 1], F32)
        g_neg = sb("g_neg", [P, 1], F32)
        stats = sb("stats", [P, NT, 6], F32)
        stats_sim = sb("stats_sim", [P, NT, 6], F32)
        mv1 = sb("mv1", [P, NT, 2], F32)
        mv2 = sb("mv2", [P, NT, 2], F32)
        ve = sb("ve", [P, NT], F32)
        rstd = sb("rstd", [P, NT], F32)
        lnb = sb("lnb", [P, NT], F32)
        lna = sb("lna", [P, NT], F32)
        ln_scale = sb("ln_scale", [P, NT], F32)
        ln_bias = sb("ln_bias", [P, NT], F32)
        ve2 = sb("ve2", [P, NT], F32)
        rstd2 = sb("rstd2", [P, NT], F32)
        nm2 = sb("nm2", [P, NT], F32)
        nmr2 = sb("nmr2", [P, NT], F32)
        minus_half = sb("minus_half", [P, NT], F32)
        ident = sb("ident", [P, P], F32)
        ones_f = sb("ones_f", [P, P], F32)
        earlier = sb("earlier", [P, P], F16)
        ones_h = sb("ones_h", [P, P], F16)
        iota_e = sb("iota_e", [P, E], F32)
        iota_lo = sb("iota_lo", [P, P], F32)
        iota_hi = sb("iota_hi", [P, E * MAXT], F32)
        id1 = sb("id1", [P, NT], F32)
        lim = sb("lim", [P, MAXT], F32)
        lmax = sb("lmax", [P, NT, 8], F32)
        lidx = sb("lidx", [P, NT, 8], U32)
        diff = sb("diff", [P, NT], F32)
        prob = sb("prob", [P, 2, NT], F32)
        idxf = sb("idxf", [P, NG, 2, TPG], F32)
        onehot = sb("onehot", [P, NG, 2, TPG, E], F32)
        picked = sb("picked", [P, NT, E], F16)
        before = sb("before", [P, NT + 1, E], F16)
        wsel = sb("wsel", [P, 2, TPG, E], F32)
        rsel = sb("rsel", [P, 2, TPG, E], F32)
        rank = sb("rank", [P, 2, TPG], F32)
        rank_i = sb("rank_i", [P, 2, TPG], I32)
        lo_i = sb("lo_i", [P, 2, TPG], I32)
        hi_i = sb("hi_i", [P, 2, TPG], I32)
        lo_f = sb("lo_f", [P, 2, TPG], F32)
        hi_f = sb("hi_f", [P, 2, TPG], F32)
        oh_lo = sb("oh_lo", [P, 2, TPG, P], F16)
        id_hi = sb("id_hi", [P, 2, TPG, E * MAXT], F16)
        idm = sb("idm", [P, E * MAXT], F32)
        pad = sb("pad", [P, E * MAXT], F32)
        gather_ids = sb("gather_ids", [P, E * MAXT + 1], U32)
        scatter_ids = sb("scatter_ids", [P, MAXT + E * MAXT + 1], U32)
        counts = sb("counts", [P, E], F32)
        over = sb("over", [P, E, MAXT - 2], F32)
        extra = sb("extra", [P, E], F32)
        extra_before = sb("extra_before", [P, E], F32)
        control = sb("control", [P, E], F32)
        ctl = sb("ctl", [P, E], I32)
        raw = [sb(f"raw{i}", [P, W_COLS], F32) for i in range(2)]
        w_hi = [sb(f"w_hi{i}", [P, W_COLS], F32R) for i in range(2)]
        w_lo = [sb(f"w_lo{i}", [P, W_COLS], F32R) for i in range(2)]
        silu = [sb(f"silu{c}", [P, FCH], F32) for c in range(2)]
        ht_hi = sb("ht_hi", [P, FB, P], F32R)
        ht_lo = sb("ht_lo", [P, FB, P], F32R)

        A = TileClass("A", sb, sem, 2)
        Bc = TileClass("B", sb, sem, 2)
        C = TileClass("C", sb, sem, 1)

        x_loaded, ctx_loaded, small_loaded = sem("x_loaded"), sem("ctx_loaded"), sem("small_loaded")
        raw_loaded = [sem(f"raw_loaded{i}") for i in range(2)]
        w_hi_ready = [sem(f"w_hi_ready{i}") for i in range(2)]
        w_lo_gu = [sem(f"w_lo_gu{i}") for i in range(2)]
        w_lo_d = [sem(f"w_lo_d{i}") for i in range(2)]
        const_step, const_ready = sem("const_step"), sem("const_ready")
        cleared = sem("cleared")
        waits_passed = sem("waits_passed")
        m_done, m_ready = sem("m_done"), sem("m_ready")
        proj_done, proj_ready = sem("proj_done"), sem("proj_ready")
        sim_done, sim_copied, sig_ready = sem("sim_done"), sem("sim_copied"), sem("sig_ready")
        sim_stats = sem("sim_stats")
        guess_ready = [sem(f"guess_ready{b}") for b in range(B)]
        signs_counted = sem("signs_counted")
        missed_ready, missed_done, general_step = sem("missed_ready"), sem("missed_done"), sem("general_step")
        missed_seen, hi_ready, id_hi_ready = sem("missed_seen"), sem("hi_ready"), sem("id_hi_ready")
        gamma_ready, gamma_parts = sem("gamma_ready"), sem("gamma_parts")
        stats1_ready, ln1_ready, base_ready = sem("stats1_ready"), sem("ln1_ready"), sem("base_ready")
        pool_step, dve_step = sem("pool_step"), sem("dve_step")
        att_ready, at_done, x2_ready = sem("att_ready"), sem("at_done"), sem("x2_ready")
        stats2_ready, ln2_ready, xn_ready = sem("stats2_ready"), sem("ln2_ready"), sem("xn_ready")
        xnt_done, xnt_ready, logits_done = sem("xnt_done"), sem("xnt_ready"), sem("logits_done")
        diff_ready, prob_ready, row_ready = sem("diff_ready"), sem("prob_ready"), sem("row_ready")
        picked_ready, rank_done, oh_lo_ready = sem("picked_ready"), sem("rank_done"), sem("oh_lo_ready")
        ids_done, counts_done, lists_ready = sem("ids_done"), sem("counts_done"), sem("lists_ready")
        x2_stored, rows_stored = sem("x2_stored"), sem("rows_stored")
        landed = sem("landed")

        block = ctx.enter_context(nc.Block())

        def piece(w, i):
            return w[:, PIECES[i][0]:PIECES[i][0] + PIECES[i][1]]

        passes = [(b, i) for first in range(0, B, 2) for i in range(STEPS_OF_GUESS) for b in (first, first + 1)]

        def own_instruction(eng):
            eng.sem_inc(waits_passed, 1)

        def load_control(eng, e):
            at = slice(e, e + 1) if isinstance(e, int) else bass.ds(e, 1)
            packed = eng.value_load(ctl[0:1, at], min_val=0, max_val=MAXT * (2 * TOK // P) + MAXT - 2)
            return packed & (MAXT - 1), packed >> LOG_MAXT

        @block.sync
        def _(sp):
            def load_expert(e, slot):
                sp.dma_start(raw[slot][:, 0:KC * F], gate[e]).then_inc(raw_loaded[slot], 16)
                sp.dma_start(raw[slot][:, KC * F:GU_COLS], up[e]).then_inc(raw_loaded[slot], 16)
                sp.dma_start(raw[slot][:, GU_COLS:W_COLS - H], down[e]).then_inc(raw_loaded[slot], 16)
                sp.dma_start(raw[slot][0:FREST, W_COLS - H:W_COLS], down_rest[e]).then_inc(raw_loaded[slot], 16)

            sp.dma_start(wq_sb[:], wq).then_inc(ctx_loaded, 16)
            sp.dma_start(wk_sb[:], wk).then_inc(ctx_loaded, 16)
            sp.dma_start(ctx_sb[:], ctxT).then_inc(ctx_loaded, 16)
            sp.dma_start(xs[:], x_view).then_inc(x_loaded, 16)
            sp.dma_start(gam[:], gamma.partition_broadcast(P)).then_inc(small_loaded, 16)
            sp.dma_start(rw[:], routerT).then_inc(small_loaded, 16)
            sp.wait_ge(cleared, 2)
            load_expert(0, 0)
            load_expert(1, 1)
            for t in (A, Bc, C):
                t.start_counts(sp)
            for g in range(NG):
                j = slice(g * TPG, (g + 1) * TPG)
                if g < NG - 1:
                    sp.wait_ge(x2_ready, BPG * (g + 1))
                    sp.dma_start(out_view[:, j, :], x2[:, j, :]).then_inc(x2_stored, 16)
                sp.wait_ge(row_ready, g + 1)
                sp.dma_start(scratch_view[:, j, :], xn[:, j, :]).then_inc(rows_stored, 16)
            with sp.Fori(0, E // 2 - 1) as q:
                for s in range(2):
                    sp.wait_ge(w_lo_gu[s], 4 * q + 4)
                    sp.wait_ge(w_lo_d[s], 2 * q + 2)
                    e = 2 * q + s + 2
                    for dst, src in ((raw[s][:, 0:KC * F], gate), (raw[s][:, KC * F:GU_COLS], up),
                                     (raw[s][:, GU_COLS:W_COLS - H], down),
                                     (raw[s][0:FREST, W_COLS - H:W_COLS], down_rest)):
                        sp.dma_start(dst, src[bass.ds(e, 1)].rearrange("a p c -> p (a c)"))\
                          .then_inc(raw_loaded[s], 16)

        @block.tensor
        def _(pe):
            def project(b):
                nc.tensor.matmul(ps[0:D, PROJ[b], 0:N], m_sb[:], ctx_sb[:, b * N:(b + 1) * N],
                                 start=True, stop=True).then_inc(proj_done, 1)

            def similarities(b):
                pe.wait_ge(proj_ready, b + 1)
                for r in range(TPB):
                    j = b * TPB + r
                    nc.tensor.matmul(ps[:, SIM[b], r * N:(r + 1) * N], mT[:, j * P:(j + 1) * P],
                                     ctx_sb[:, b * N:(b + 1) * N], start=True, stop=True).then_inc(sim_done, 1)

            pe.wait_ge(ctx_loaded, 48)
            nc.tensor.matmul(ps[0:D, PROJ[0], N:N + D], wq_sb[:], wk_sb[:], start=True, stop=True).then_inc(m_done, 1)
            pe.wait_ge(m_ready, 1)
            project(0)
            for b in range(B):
                if b < B - 1:
                    project(b + 1)
                similarities(b)
            pe.wait_ge(const_ready, 1)
            pe.wait_ge(small_loaded, 32)
            pe.wait_ge(missed_ready, 1)
            nc.tensor.matmul(ps[:, IDS, 0:1], ones_f[:], missed_sum[:], start=True, stop=True).then_inc(missed_done, 1)

            def transpose_a(g):
                for b in range(g * BPG, (g + 1) * BPG):
                    pe.wait_ge(att_ready, TPB * (b + 1))
                    for r in range(TPB):
                        for c in range(TPB):
                            last = nc.tensor.transpose(ps[:, SIM[b], r * N + c * P:r * N + (c + 1) * P],
                                                       att[:, b * TPB + c, r * P:(r + 1) * P], ident[:])
                    last.then_inc(at_done, 1)

            def logits(g):
                pe.wait_ge(xn_ready, TPG * (g + 1))
                if g:
                    pe.wait_ge(xnt_ready, BPG * g)
                for b in range(BPG):
                    for r in range(TPB):
                        for k in range(KC):
                            last = nc.tensor.transpose(ps[:, XNT[b], (r * KC + k) * P:(r * KC + k + 1) * P],
                                                       xn[:, g * TPG + b * TPB + r, k * P:(k + 1) * P], ident[:])
                    last.then_inc(xnt_done, 1)
                if g:
                    pe.wait_ge(oh_lo_ready, g)
                for b in range(BPG):
                    pe.wait_ge(xnt_ready, BPG * g + b + 1)
                    for r in range(b * TPB, (b + 1) * TPB):
                        for k in range(KC):
                            last = nc.tensor.matmul(ps[:, LOG, r * E:(r + 1) * E], xnT[:, r, k, :], rw[:, k, :],
                                                    start=(k == 0), stop=(k == KC - 1))
                last.then_inc(logits_done, 1)

            def ranks(g):
                pe.wait_ge(picked_ready, g + 1)
                j = slice(g * TPG, (g + 1) * TPG)
                o = ps[:, LOG, 64:64 + TPG * E]
                nc.tensor.matmul(o, earlier[:], picked[:, j, :].rearrange("p j e -> p (j e)"), start=True, stop=False)
                nc.tensor.matmul(o, ones_h[:], before[:, j, :].rearrange("p j e -> p (j e)"),
                                 start=False, stop=True).then_inc(rank_done, 1)
                if g == NG - 1:
                    nc.tensor.matmul(ps[:, LOG, 128:128 + E], ones_h[:], before[:, NT, :],
                                     start=True, stop=True).then_inc(counts_done, 1)

            def token_ids(g):
                if g == 0:
                    pe.wait_ge(missed_seen, 1)
                pe.wait_ge(oh_lo_ready, g + 1)
                pe.wait_ge(id_hi_ready, g + 1)
                for c in range(2):
                    for r in range(TPG):
                        last = nc.tensor.matmul(ps[:, IDS, 0:E * MAXT], oh_lo[:, c, r, :], id_hi[:, c, r, :],
                                                start=(g == 0 and c == 0 and r == 0),
                                                stop=(g == NG - 1 and c == 1 and r == TPG - 1))
                last.then_inc(ids_done, 1)

            for g in range(NG):
                transpose_a(g)
            for g in range(NG):
                logits(g)
                ranks(g)
                token_ids(g)

            pe.wait_ge(lists_ready, 3)

            def x_transpose(t, n, slot, gathers):
                pe.wait_ge(t.gathered[slot], 16 * gathers)
                for k in range(KC):
                    last = nc.tensor.transpose(ps[:, XB, k * P:(k + 1) * P], t.xg[slot][:, k * P:(k + 1) * P], ident[:])
                last.then_inc(t.x_transposed, 1)

            def gate_up(t, n, c, s):
                if c == 0:
                    pe.wait_ge(t.x_ready, after(n + 1))
                for bank, m in ((GB[c], 0), (UB[c], 1)):
                    for k in range(KC):
                        lo = (m * KC + k) * F + c * FCH
                        hi_w, lo_w = w_hi[s][:, lo:lo + FCH], w_lo[s][:, lo:lo + FCH]
                        o = ps[:, bank, 0:FCH]
                        nc.tensor.matmul(o, t.xt_hi[:, k, :], hi_w, start=(k == 0), stop=False)
                        nc.tensor.matmul(o, t.xt_hi[:, k, :], lo_w, start=False, stop=False)
                        last = nc.tensor.matmul(o, t.xt_lo[:, k, :], hi_w, start=False, stop=(k == KC - 1))
                last.then_inc(t.gu_done[c], 1)

            def h_transpose(t, n):
                for i, blocks in enumerate((range(0, 4), range(4, FB))):
                    pe.wait_ge(t.h_ready[1 - i], after(n + 1))
                    for f in blocks:
                        last = nc.tensor.transpose(ps[:, TB[i], (f % 4) * P:(f % 4 + 1) * P],
                                                   t.h[:, f * P:(f + 1) * P], ident[:])
                    last.then_inc(t.h_transposed[i], 1)

            def down_product(t, n, s):
                o = ps[:, YB, 0:H]
                for f in range(FB):
                    if f == 0:
                        pe.wait_ge(t.ht_ready[0], after(n + 1))
                    if f == 4:
                        pe.wait_ge(t.ht_ready[1], after(n + 1))
                    lo = GU_COLS + f * H
                    hi_w, lo_w = w_hi[s][:, lo:lo + H], w_lo[s][:, lo:lo + H]
                    nc.tensor.matmul(o, ht_hi[:, f, :], hi_w, start=(f == 0), stop=False)
                    nc.tensor.matmul(o, ht_hi[:, f, :], lo_w, start=False, stop=False)
                    last = nc.tensor.matmul(o, ht_lo[:, f, :], hi_w, start=False, stop=(f == FB - 1))
                last.then_inc(t.down_done, 1)

            def expert(q, s, last):
                e = 2 * q + s
                extras, so_far = load_control(pe, e)
                pe.wait_ge(w_lo_gu[s], 4 * q + 4)

                def previous_b_transpose():
                    h_transpose(Bc, e - 1)

                def previous_b_down():
                    pe.wait_ge(A.y_ready, after(e))
                    pe.wait_ge(C.y_ready, after(so_far))
                    down_product(Bc, e - 1, 1 - s)

                pe.wait_ge(A.x_ready, after(e + 1))
                x_transpose(Bc, e, s, q + 1)
                pe.wait_ge(Bc.h_ready[0], after(e))
                gate_up(A, e, 0, s)
                if s == 0:
                    with pe.If(q > 0):
                        previous_b_transpose()
                else:
                    previous_b_transpose()
                pe.wait_ge(Bc.h_ready[1], after(e))
                gate_up(A, e, 1, s)

                def b_down():
                    if s == 0:
                        with pe.If(q > 0):
                            previous_b_down()
                    else:
                        previous_b_down()

                def next_a():
                    if not last:
                        pe.wait_ge(Bc.x_ready, after(e + 1))
                        x_transpose(A, e + 1, 1 - s, q + 1 + s)

                with pe.If(extras > 0):
                    n = so_far
                    pe.wait_ge(Bc.x_ready, after(e + 1))
                    x_transpose(C, n, 0, n + 1)
                    b_down()
                    h_transpose(A, e)
                    gate_up(C, n, 0, s)
                    pe.wait_ge(Bc.y_ready, after(e))
                    pe.wait_ge(w_lo_d[s], 2 * q + 2)
                    down_product(A, e, s)
                    gate_up(C, n, 1, s)
                    next_a()
                    pe.wait_ge(C.h_ready[0], after(n + 1))
                    gate_up(Bc, e, 0, s)
                    h_transpose(C, n)
                    gate_up(Bc, e, 1, s)
                    pe.wait_ge(A.y_ready, after(e + 1))
                    down_product(C, n, s)
                    if not last:
                        pe.wait_ge(A.x_ready, after(e + 2))
                    with pe.If(extras > 1):
                        pe.wait_ge(Bc.h_ready[0], after(e + 1))
                        pe.wait_ge(Bc.h_ready[1], after(e + 1))
                        own_instruction(pe)
                        with pe.Fori(1, extras) as t:
                            n = so_far + t
                            pe.wait_ge(C.y_ready, after(n))
                            x_transpose(C, n, 0, n + 1)
                            gate_up(C, n, 0, s)
                            gate_up(C, n, 1, s)
                            h_transpose(C, n)
                            down_product(C, n, s)
                with pe.Else():
                    b_down()
                    h_transpose(A, e)
                    next_a()
                    gate_up(Bc, e, 0, s)
                    if last:
                        gate_up(Bc, e, 1, s)
                    pe.wait_ge(Bc.y_ready, after(e))
                    pe.wait_ge(w_lo_d[s], 2 * q + 2)
                    down_product(A, e, s)
                    if not last:
                        gate_up(Bc, e, 1, s)

            x_transpose(A, 0, 0, 1)
            with pe.Fori(0, E // 2 - 1) as q:
                expert(q, 0, False)
                expert(q, 1, False)
            expert(E // 2 - 1, 0, False)
            expert(E // 2 - 1, 1, True)
            h_transpose(Bc, E - 1)
            extras, so_far = load_control(pe, E - 1)
            pe.wait_ge(A.y_ready, after(E))
            pe.wait_ge(C.y_ready, after(so_far + extras))
            down_product(Bc, E - 1, 1)

        @block.scalar
        def _(act):
            for b, i in passes:
                act.wait_ge(guess_ready[b], i + 1)
                for r in range(TPB):
                    j = b * TPB + r
                    nc.scalar.activation(att[:, j, :], sim[:, j, :], ACT.Sign, scale=-1.0, bias=guess[:, j:j + 1],
                                         accum_out=signs[:, j:j + 1]).then_inc(signs_counted, 1)
            act.wait_ge(small_loaded, 32)
            nc.scalar.activation(g_full[:], gam[:], ACT.Sigmoid).then_inc(gamma_ready, 1)
            act.wait_ge(signs_counted, TPB * len(passes))
            for b in range(B):
                j = slice(b * TPB, (b + 1) * TPB)
                nc.scalar.activation(att[:, j, :], sim[:, j, :], ACT.Sigmoid).then_inc(sig_ready, 1)
            act.wait_ge(raw_loaded[0], 64)
            for i in range(len(PIECES)):
                nc.scalar.activation(piece(w_hi[0], i), piece(raw[0], i), ACT.Copy).then_inc(w_hi_ready[0], 1)
            act.wait_ge(ln1_ready, 2)
            for j in range(NT):
                nc.scalar.activation(xs[:, j, :], xs[:, j, :], ACT.Identity, scale=ln_scale[:, j:j + 1],
                                     bias=ln_bias[:, j:j + 1]).then_inc(base_ready, 1)
            for g in range(NG):
                act.wait_ge(ln2_ready, g + 1)
                for j in range(g * TPG, (g + 1) * TPG):
                    nc.scalar.activation(xn[:, j, 0:H], x2[:, j, :], ACT.Identity, scale=rstd2[:, j:j + 1],
                                         bias=nmr2[:, j:j + 1]).then_inc(xn_ready, 1)
                if g:
                    act.wait_ge(logits_done, g)
                for b in range(BPG):
                    act.wait_ge(xnt_done, BPG * g + b + 1)
                    nc.scalar.activation(xnT[:, b * TPB:(b + 1) * TPB],
                                         ps[:, XNT[b], :].rearrange("p (r k t) -> p r k t", r=TPB, k=KC), ACT.Copy)\
                      .then_inc(xnt_ready, 1)
                act.wait_ge(diff_ready, g + 1)
                j = slice(g * TPG, (g + 1) * TPG)
                nc.scalar.activation(prob[:, 0, j], diff[:, j], ACT.Sigmoid).then_inc(prob_ready, 1)
                nc.scalar.activation(prob[:, 1, j], diff[:, j], ACT.Sigmoid, scale=-1.0).then_inc(prob_ready, 1)

            def x_hi(t, n):
                act.wait_ge(t.x_transposed, after(n + 1))
                nc.scalar.copy(t.xt_hi[:], ps[:, XB, 0:H].rearrange("p (k t) -> p k t", k=KC))\
                  .then_inc(t.x_hi_ready, 1)

            def gate_silu(t, n, c):
                act.wait_ge(t.gu_done[c], after(n + 1))
                nc.scalar.activation(silu[c][:], ps[:, GB[c], 0:FCH], ACT.Silu).then_inc(t.silu_ready[c], 1)

            def ht_high(t, n):
                for i, (f0, f1) in enumerate(((0, 4), (4, FB))):
                    act.wait_ge(t.h_transposed[i], after(n + 1))
                    nc.scalar.copy(ht_hi[:, f0:f1, :],
                                   ps[:, TB[i], 0:(f1 - f0) * P].rearrange("p (f t) -> p f t", t=P)).then_inc(t.ht_hi_ready[i], 1)

            def expert(q, s, last):
                e = 2 * q + s
                extras, so_far = load_control(act, e)

                def split_next(*pieces):
                    if last:
                        return
                    for i in pieces:
                        if i == 0:
                            act.wait_ge(raw_loaded[1 - s], 64 * (q + s + 1))
                            act.wait_ge(Bc.gu_done[1], after(e))
                            act.wait_ge(C.gu_done[1], after(so_far))
                        if i == len(GU_PIECES):
                            act.wait_ge(Bc.down_done, after(e))
                            act.wait_ge(C.down_done, after(so_far))
                        nc.scalar.copy(piece(w_hi[1 - s], i), piece(raw[1 - s], i))\
                          .then_inc(w_hi_ready[1 - s], 1)

                x_hi(Bc, e)
                gate_silu(A, e, 0)
                split_next(0)
                if s == 0:
                    with act.If(q > 0):
                        ht_high(Bc, e - 1)
                else:
                    ht_high(Bc, e - 1)
                split_next(1)
                gate_silu(A, e, 1)
                with act.If(extras > 0):
                    n = so_far
                    x_hi(C, n)
                    ht_high(A, e)
                    gate_silu(C, n, 0)
                    split_next(2)
                    gate_silu(C, n, 1)
                    if not last:
                        x_hi(A, e + 1)
                    split_next(3)
                    gate_silu(Bc, e, 0)
                    ht_high(C, n)
                with act.Else():
                    ht_high(A, e)
                    if not last:
                        x_hi(A, e + 1)
                    split_next(2)
                    gate_silu(Bc, e, 0)
                    split_next(3)
                split_next(4)
                gate_silu(Bc, e, 1)
                split_next(5)
                with act.If(extras > 1):
                    with act.Fori(1, extras) as t:
                        n = so_far + t
                        x_hi(C, n)
                        gate_silu(C, n, 0)
                        gate_silu(C, n, 1)
                        ht_high(C, n)

            nc.scalar.preload_act_table(ACT.Silu)
            act.wait_ge(lists_ready, 3)
            x_hi(A, 0)
            with act.Fori(0, E // 2 - 1) as q:
                expert(q, 0, False)
                expert(q, 1, False)
            expert(E // 2 - 1, 0, False)
            expert(E // 2 - 1, 1, True)
            ht_high(Bc, E - 1)

        @block.vector
        def _(dve):
            steps = [0]

            def step(ins):
                steps[0] += 1
                ins.then_inc(dve_step, 1)
                dve.wait_ge(dve_step, steps[0])

            for s in range(2):
                nc.vector.memset(raw[s][:, W_COLS - H:W_COLS], 0.0).then_inc(cleared, 1)
            for t in (A, Bc, C):
                nc.vector.memset(t.h[:, F:FB * P], 0.0).then_inc(cleared, 1)
            step(nc.vector.memset(before[:, 0, :], 0.0))

            def projected(b):
                dve.wait_ge(proj_done, b + 1)
                nc.vector.tensor_scalar(mT[:, b * N:(b + 1) * N], ps[0:D, PROJ[b], 0:N], 1.0 / 16.0, None, ALU.mult)\
                  .then_inc(proj_ready, 1)

            def copy_sim(b):
                dve.wait_ge(sim_done, TPB * (b + 1))
                j = slice(b * TPB, (b + 1) * TPB)
                nc.vector.tensor_copy(sim[:, j, :], ps[:, SIM[b], :].rearrange("p (r n) -> p r n", r=TPB))\
                  .then_inc(sim_copied, 1)
                dve.wait_ge(sim_copied, b + 1)
                for r in range(TPB):
                    nc.vector.bn_stats(stats_sim[:, b * TPB + r, :], sim[:, b * TPB + r, :]).then_inc(dve_step, 1)
                steps[0] += TPB
                dve.wait_ge(dve_step, steps[0])
                for r in range(TPB):
                    nc.vector.bn_aggr(mvs[:, b * TPB + r, :], stats_sim[:, b * TPB + r, :]).then_inc(sim_stats, 1)

            def both(*makers):
                done = [0] * TPB
                for make in makers:
                    for r in range(TPB):
                        if done[r]:
                            dve.wait_ge(dve_step, done[r])
                        make(r).then_inc(dve_step, 1)
                        steps[0] += 1
                        done[r] = steps[0]
                dve.wait_ge(dve_step, steps[0])

            def find_threshold(b):
                t = b * TPB
                dve.wait_ge(guess_ready[b], STEPS_OF_GUESS + 1)
                both(lambda r: nc.vector.tensor_scalar(work[:, r, :], sim[:, t + r, :], guess[:, t + r:t + r + 1], None,
                                                       ALU.is_ge, ALU.add, accum_out=above[:, t + r:t + r + 1]),
                     lambda r: nc.vector.scalar_tensor_tensor(work[:, r, :], work[:, r, :], -3e38, sim[:, t + r, :],
                                                              ALU.mult, ALU.add),
                     lambda r: nc.vector.max(top[:, t + r, 0:8], work[:, r, :]),
                     lambda r: nc.vector.match_replace(work[:, r, :], top[:, t + r, 0:8], work[:, r, :], LOWEST),
                     lambda r: nc.vector.max(top[:, t + r, 8:WINDOW], work[:, r, :]))

            def choose():
                nc.vector.tensor_scalar(wanted[:], above[:], -1.0, KTOP - 1.0, ALU.mult, ALU.add).then_inc(dve_step, 1)
                nc.vector.tensor_scalar(off[:], above[:], 1.0, -COUNT_MID, ALU.mult, ALU.add).then_inc(dve_step, 1)
                steps[0] += 2
                dve.wait_ge(dve_step, steps[0])
                step(nc.vector.tensor_tensor(off_squared[:], off[:], off[:], ALU.mult))
                step(nc.vector.tensor_scalar(missed[:], off_squared[:], (WINDOW / 2) ** 2, None, ALU.is_gt, ALU.add,
                                             accum_out=missed_sum[:]))
                nc.vector.sem_inc(missed_ready, 1)
                for j in range(NT):
                    nc.vector.scalar_tensor_tensor(chosen[:, j, :], iota_lo[:, 0:WINDOW], wanted[:, j:j + 1],
                                                   top[:, j, :], ALU.is_equal, ALU.mult,
                                                   accum_out=threshold[:, j:j + 1]).then_inc(dve_step, 1)
                steps[0] += NT
                dve.wait_ge(dve_step, steps[0])

            def thresholds_in_general():
                per_tile = 2 * ROUNDS + 1
                dve.sem_inc(general_step, 1)
                with dve.Fori(0, NT) as j:
                    count = [per_tile * j + 1]

                    def in_turn():
                        dve.wait_ge(general_step, count[0])
                        own_instruction(dve)
                        count[0] = count[0] + 1

                    in_turn()
                    nc.vector.tensor_copy(work1[:], sim[:, bass.ds(j, 1), :].rearrange("p a n -> p (a n)"))\
                      .then_inc(general_step, 1)
                    for i in range(ROUNDS):
                        in_turn()
                        nc.vector.max(top1[:], work1[:]).then_inc(general_step, 1)
                        if i < ROUNDS - 1:
                            in_turn()
                            nc.vector.match_replace(work1[:], top1[:], work1[:], LOWEST).then_inc(general_step, 1)
                    in_turn()
                    last_kept = (KTOP - 1) % 8
                    nc.vector.tensor_copy(threshold[:, bass.ds(j, 1)], top1[:, last_kept:last_kept + 1])\
                      .then_inc(general_step, 1)
                dve.wait_ge(general_step, per_tile * NT + 1)

            def mask(b):
                dve.wait_ge(sig_ready, b + 1)
                for j in range(b * TPB, (b + 1) * TPB):
                    nc.vector.scalar_tensor_tensor(att[:, j, :], sim[:, j, :], threshold[:, j:j + 1],
                                                   att[:, j, :], ALU.is_ge, ALU.mult).then_inc(att_ready, 1)

            def residual(b):
                j = slice(b * TPB, (b + 1) * TPB)
                dve.wait_ge(att_ready, TPB * (b + 1))
                dve.wait_ge(base_ready, TPB * (b + 1))
                dve.wait_ge(gamma_parts, 3)
                step(nc.vector.scalar_tensor_tensor(xs[:, j, :], att[:, j, :], g_half[:, 0:1], xs[:, j, :],
                                                    ALU.mult, ALU.add))
                dve.wait_ge(at_done, b + 1)
                nc.vector.scalar_tensor_tensor(x2[:, j, :], ps[:, SIM[b], :].rearrange("p (r n) -> p r n", r=TPB),
                                               g_half[:, 0:1], xs[:, j, :], ALU.mult, ALU.add).then_inc(x2_ready, 1)
                dve.wait_ge(x2_ready, b + 1)
                for r in range(TPB):
                    nc.vector.bn_stats(stats[:, b * TPB + r, :], x2[:, b * TPB + r, :]).then_inc(dve_step, 1)
                steps[0] += TPB
                dve.wait_ge(dve_step, steps[0])
                for r in range(TPB):
                    nc.vector.bn_aggr(mv2[:, b * TPB + r, :], stats[:, b * TPB + r, :]).then_inc(stats2_ready, 1)

            def pick(g):
                dve.wait_ge(logits_done, g + 1)
                for r in range(TPG):
                    nc.vector.max(lmax[:, g * TPG + r, :], ps[:, LOG, r * E:(r + 1) * E]).then_inc(dve_step, 1)
                steps[0] += TPG
                dve.wait_ge(dve_step, steps[0])
                j = slice(g * TPG, (g + 1) * TPG)
                nc.vector.tensor_tensor(diff[:, j], lmax[:, j, 0], lmax[:, j, 1], ALU.subtract).then_inc(diff_ready, 1)
                for r in range(TPG):
                    nc.vector.max_index(lidx[:, g * TPG + r, :], lmax[:, g * TPG + r, :],
                                        ps[:, LOG, r * E:(r + 1) * E]).then_inc(dve_step, 1)
                steps[0] += TPG
                dve.wait_ge(dve_step, steps[0])
                step(nc.vector.tensor_copy(idxf[:, g], lidx[:, j, 0:2].rearrange("p j c -> p c j")))
                dve.wait_ge(const_ready, 1)
                bc = [P, 2, TPG, E]
                step(nc.vector.tensor_tensor(onehot[:, g], iota_e[:, None, None, :].to_broadcast(bc),
                                             idxf[:, g, :, :, None].to_broadcast(bc), ALU.is_equal))
                step(nc.vector.tensor_tensor(picked[:, j, :], onehot[:, g, 0], onehot[:, g, 1], ALU.add))
                for r in range(TPG):
                    t = g * TPG + r
                    ins = nc.vector.tensor_tensor(before[:, t + 1, :], before[:, t, :], picked[:, t, :], ALU.add)
                    if r < TPG - 1:
                        step(ins)
                    else:
                        ins.then_inc(picked_ready, 1)
                dve.wait_ge(picked_ready, g + 1)
                dve.wait_ge(prob_ready, 2 * (g + 1))
                step(nc.vector.tensor_tensor(wsel[:], onehot[:, g], prob[:, :, j][:, :, :, None].to_broadcast(bc),
                                             ALU.mult))
                nc.vector.tensor_tensor(xn[:, j, H:ROW], wsel[:, 0], wsel[:, 1], ALU.add).then_inc(row_ready, 1)

            def place(g):
                dve.wait_ge(rank_done, g + 1)
                if g:
                    dve.wait_ge(ids_done, g)
                bc = [P, 2, TPG, E]
                step(nc.vector.tensor_tensor(
                    rsel[:], onehot[:, g],
                    ps[:, LOG, 64:64 + TPG * E].rearrange("p (r e) -> p r e", e=E)[:, None].to_broadcast(bc), ALU.mult))
                step(nc.vector.tensor_reduce(rank[:], rsel[:], AX.X, ALU.add))
                step(nc.vector.tensor_copy(rank_i[:], rank[:]))
                nc.vector.tensor_single_scalar(hi_i[:], rank_i[:], 7, ALU.arith_shift_right).then_inc(dve_step, 1)
                nc.vector.tensor_single_scalar(lo_i[:], rank_i[:], P - 1, ALU.bitwise_and).then_inc(dve_step, 1)
                steps[0] += 2
                dve.wait_ge(dve_step, steps[0])
                nc.vector.scalar_tensor_tensor(hi_f[:], idxf[:, g], float(MAXT), hi_i[:], ALU.mult, ALU.add)\
                  .then_inc(hi_ready, 1)
                step(nc.vector.tensor_copy(lo_f[:], lo_i[:]))
                for c in range(2):
                    for r in range(TPG):
                        last = nc.vector.tensor_scalar(oh_lo[:, c, r, :], iota_lo[:], lo_f[:, c, r:r + 1], None,
                                                       ALU.is_equal)
                last.then_inc(oh_lo_ready, 1)

            dve.wait_ge(m_done, 1)
            nc.vector.tensor_copy(m_sb[:], ps[0:D, PROJ[0], N:N + D]).then_inc(m_ready, 1)
            projected(0)
            for b in range(B):
                if b < B - 1:
                    projected(b + 1)
                copy_sim(b)
            dve.wait_ge(const_ready, 1)
            for b in range(B):
                find_threshold(b)
                if b == 0:
                    dve.wait_ge(x_loaded, 16)
                    for j in range(NT):
                        nc.vector.bn_stats(stats[:, j, :], xs[:, j, :]).then_inc(dve_step, 1)
                    steps[0] += NT
                    dve.wait_ge(dve_step, steps[0])
                    for j in range(NT):
                        nc.vector.bn_aggr(mv1[:, j, :], stats[:, j, :]).then_inc(stats1_ready, 1)
            choose()
            dve.wait_ge(missed_done, 1)
            nc.vector.tensor_scalar(missed_any[:], ps[:, IDS, 0:1], 1.0, None, ALU.min).then_inc(missed_seen, 1)
            dve.wait_ge(missed_seen, 1)
            missed_rows = dve.value_load(missed_any[0:1, 0:1], min_val=0, max_val=1)
            with dve.If(missed_rows > 0):
                thresholds_in_general()
            for g in range(NG):
                for b in range(g * BPG, (g + 1) * BPG):
                    mask(b)
                for b in range(g * BPG, (g + 1) * BPG):
                    residual(b)
            for g in range(NG):
                pick(g)
                if g < NG - 1:
                    place(g)
            dve.wait_ge(counts_done, 1)
            step(nc.vector.tensor_copy(counts[:], ps[:, LOG, 128:128 + E]))
            bc = [P, E, MAXT - 2]
            step(nc.vector.tensor_tensor(over[:], counts[:, :, None].to_broadcast(bc),
                                         lim[:, None, 2:MAXT].to_broadcast(bc), ALU.is_gt))
            step(nc.vector.tensor_reduce(extra[:], over[:], AX.X, ALU.add))
            step(nc.vector.memset(extra_before[:, 0:1], 0.0))
            for e in range(1, E):
                step(nc.vector.tensor_tensor(extra_before[:, e:e + 1], extra_before[:, e - 1:e], extra[:, e - 1:e],
                                             ALU.add))
            step(nc.vector.scalar_tensor_tensor(control[:], extra_before[:], float(MAXT), extra[:], ALU.mult, ALU.add))
            nc.vector.tensor_copy(ctl[:], control[:]).then_inc(lists_ready, 1)
            place(NG - 1)
            dve.wait_ge(ids_done, NG)
            nc.vector.tensor_scalar(idm[:], ps[:, IDS, 0:E * MAXT], -1.0, 0.0, ALU.add, ALU.max).then_inc(dve_step, 1)
            nc.vector.tensor_scalar(pad[:], ps[:, IDS, 0:E * MAXT], 0.0, SKIP, ALU.is_equal, ALU.mult)\
              .then_inc(dve_step, 1)
            steps[0] += 2
            dve.wait_ge(dve_step, steps[0])
            nc.vector.tensor_copy(gather_ids[:, 0:E * MAXT], idm[:]).then_inc(lists_ready, 1)
            nc.vector.tensor_tensor(scatter_ids[:, MAXT:MAXT + E * MAXT], idm[:], pad[:], ALU.add).then_inc(lists_ready, 1)
            dve.wait_ge(lists_ready, 3)

            def x_lo(t, n, slot, e):
                dve.wait_ge(t.x_hi_ready, after(n + 1))
                nc.vector.tensor_copy(t.weight[slot][:], t.xg[slot][:, bass.ds(H + e, 1)]).then_inc(t.weight_ready, 1)
                nc.vector.tensor_tensor(t.xt_lo[:], ps[:, XB, 0:H].rearrange("p (k t) -> p k t", k=KC),
                                        t.xt_hi[:].bitcast(F32), ALU.subtract).then_inc(t.x_ready, 1)

            def hidden(t, n, c):
                dve.wait_ge(t.silu_ready[c], after(n + 1))
                dve.wait_ge(t.h_transposed[1], after(n))
                nc.vector.tensor_tensor(t.h[:, c * FCH:(c + 1) * FCH], silu[c][:], ps[:, UB[c], 0:FCH],
                                        ALU.mult).then_inc(t.h_ready[c], 1)

            def ht_low(t, n):
                for i, (f0, f1) in enumerate(((0, 4), (4, FB))):
                    dve.wait_ge(t.ht_hi_ready[i], after(n + 1))
                    nc.vector.tensor_tensor(ht_lo[:, f0:f1, :],
                                            ps[:, TB[i], 0:(f1 - f0) * P].rearrange("p (f t) -> p f t", t=P),
                                            ht_hi[:, f0:f1, :].bitcast(F32), ALU.subtract).then_inc(t.ht_ready[i], 1)

            def weigh(t, n, slot, later, listed):
                dve.wait_ge(t.down_done, after(n + 1))
                dve.wait_ge(later.to_listed, after(listed))
                nc.vector.tensor_scalar(t.y[:], ps[:, YB, 0:H], t.weight[slot][:, 0:1], None,
                                        ALU.mult).then_inc(t.y_ready, 1)

            def expert(q, s, last):
                e = 2 * q + s
                extras, so_far = load_control(dve, e)

                def split_next(*pieces):
                    if last:
                        return
                    for i in pieces:
                        dve.wait_ge(w_hi_ready[1 - s], len(PIECES) * (q + s) + i + 1)
                        nc.vector.tensor_tensor(piece(w_lo[1 - s], i), piece(raw[1 - s], i),
                                                piece(w_hi[1 - s], i).bitcast(F32), ALU.subtract)\
                          .then_inc((w_lo_gu if i < len(GU_PIECES) else w_lo_d)[1 - s], 1)

                x_lo(Bc, e, s, e)
                hidden(A, e, 0)
                if s == 0:
                    with dve.If(q > 0):
                        ht_low(Bc, e - 1)
                else:
                    ht_low(Bc, e - 1)
                split_next(1)
                hidden(A, e, 1)

                def weigh_b():
                    if s == 0:
                        with dve.If(q > 0):
                            weigh(Bc, e - 1, 1 - s, A, e)
                    else:
                        weigh(Bc, e - 1, 1 - s, A, e)

                with dve.If(extras > 0):
                    n = so_far
                    x_lo(C, n, 0, e)
                    weigh_b()
                    ht_low(A, e)
                    hidden(C, n, 0)
                    weigh(A, e, s, Bc, e)
                    split_next(2)
                    hidden(C, n, 1)
                    if not last:
                        x_lo(A, e + 1, 1 - s, e + 1)
                    hidden(Bc, e, 0)
                    ht_low(C, n)
                    split_next(3)
                    hidden(Bc, e, 1)
                    weigh(C, n, 0, Bc, e)
                with dve.Else():
                    weigh_b()
                    ht_low(A, e)
                    if not last:
                        x_lo(A, e + 1, 1 - s, e + 1)
                    split_next(2)
                    hidden(Bc, e, 0)
                    split_next(3)
                    if last:
                        hidden(Bc, e, 1)
                    weigh(A, e, s, Bc, e)
                    if not last:
                        hidden(Bc, e, 1)
                split_next(5)
                with dve.If(extras > 1):
                    with dve.Fori(1, extras) as t:
                        n = so_far + t
                        x_lo(C, n, 0, e)
                        hidden(C, n, 0)
                        hidden(C, n, 1)
                        ht_low(C, n)
                        weigh(C, n, 0, C, n + 1)

            x_lo(A, 0, 0, 0)
            with dve.Fori(0, E // 2 - 1) as q:
                expert(q, 0, False)
                expert(q, 1, False)
            expert(E // 2 - 1, 0, False)
            expert(E // 2 - 1, 1, True)
            ht_low(Bc, E - 1)
            weigh(Bc, E - 1, 1, A, E)

        @block.gpsimd
        def _(pool):
            steps = [0]

            def step(ins):
                steps[0] += 1
                ins.then_inc(pool_step, 1)
                pool.wait_ge(pool_step, steps[0])

            nc.gpsimd.memset(ones_f[:], 1.0).then_inc(const_step, 1)
            nc.gpsimd.memset(ones_h[:], 1.0).then_inc(const_step, 1)
            nc.gpsimd.memset(minus_half[:], -0.5).then_inc(const_step, 1)
            nc.gpsimd.memset(half[:], 0.5).then_inc(const_step, 1)
            pool.wait_ge(const_step, 4)
            nc.gpsimd.affine_select(out=ident[:], in_=ones_f[:], compare_op=ALU.is_equal, fill=0.0, base=0,
                                    pattern=[[-1, P]], channel_multiplier=1).then_inc(const_step, 1)
            nc.gpsimd.affine_select(out=earlier[:], in_=ones_h[:], compare_op=ALU.is_gt, fill=0.0, base=0,
                                    pattern=[[1, P]], channel_multiplier=-1).then_inc(const_step, 1)
            imprecise = dict(allow_small_or_imprecise_dtypes=True)
            nc.gpsimd.iota(iota_e[:], pattern=[[1, E]], base=0, channel_multiplier=0, **imprecise).then_inc(const_step, 1)
            nc.gpsimd.iota(iota_lo[:], pattern=[[1, P]], base=0, channel_multiplier=0, **imprecise).then_inc(const_step, 1)
            nc.gpsimd.iota(iota_hi[:], pattern=[[1, E * MAXT]], base=0, channel_multiplier=0, **imprecise)\
              .then_inc(const_step, 1)
            nc.gpsimd.iota(id1[:], pattern=[[P, NT]], base=1, channel_multiplier=1, **imprecise).then_inc(const_step, 1)
            nc.gpsimd.iota(lim[:], pattern=[[P, MAXT]], base=0, channel_multiplier=0, **imprecise).then_inc(const_step, 1)
            pool.wait_ge(const_step, 11)
            pool.sem_inc(const_ready, 1)

            def first_guess(b):
                t = slice(b * TPB, (b + 1) * TPB)
                pool.wait_ge(sim_stats, TPB * (b + 1))
                step(nc.gpsimd.tensor_tensor(deviation[:, t], mvs[:, t, 1], half[:, t], ALU.pow))
                for j in range(b * TPB, (b + 1) * TPB):
                    last = nc.gpsimd.tensor_scalar(guess[:, j:j + 1], deviation[:, j:j + 1], half[:, 0:1],
                                                   mvs[:, j, 0:1], ALU.mult, ALU.add)
                    last.then_inc(pool_step, 1)
                steps[0] += TPB
                pool.wait_ge(pool_step, steps[0])
                pool.sem_inc(guess_ready[b], 1)
                nc.gpsimd.tensor_scalar(slope[:, t], deviation[:, t], -0.5 / GUESS_DENSITY, 0.0, ALU.mult, ALU.add)\
                  .then_inc(pool_step, 1)
                nc.gpsimd.tensor_scalar(slope_base[:, t], deviation[:, t], (N / 2 - TARGET) / GUESS_DENSITY, 0.0,
                                        ALU.mult, ALU.add).then_inc(pool_step, 1)
                steps[0] += 2
                pool.wait_ge(pool_step, steps[0])
                nc.gpsimd.tensor_tensor(guess_base[:, t], guess[:, t], slope_base[:, t], ALU.add)\
                  .then_inc(pool_step, 1)
                steps[0] += 1

            def next_guess(b, i):
                t = slice(b * TPB, (b + 1) * TPB)
                pool.wait_ge(pool_step, steps[0])
                for j in range(b * TPB, (b + 1) * TPB):
                    nc.gpsimd.tensor_scalar(guess[:, j:j + 1], signs[:, j:j + 1], slope[:, j:j + 1],
                                            guess_base[:, j:j + 1], ALU.mult, ALU.add).then_inc(pool_step, 1)
                steps[0] += TPB
                pool.wait_ge(pool_step, steps[0])
                pool.sem_inc(guess_ready[b], 1)
                if i < STEPS_OF_GUESS - 1:
                    nc.gpsimd.tensor_tensor(guess_base[:, t], guess[:, t], slope_base[:, t], ALU.add)\
                      .then_inc(pool_step, 1)
                    steps[0] += 1

            first_guess(0)
            first_guess(1)
            for at, (b, i) in enumerate(passes):
                if at == 4:
                    first_guess(2)
                    first_guess(3)
                pool.wait_ge(signs_counted, TPB * (at + 1))
                next_guess(b, i)
            pool.wait_ge(gamma_ready, 1)
            nc.gpsimd.tensor_scalar(g_half[:], g_full[:], 0.5, 0.0, ALU.mult, ALU.add).then_inc(gamma_parts, 1)
            nc.gpsimd.tensor_scalar(g_rest[:], g_full[:], -1.0, 1.0, ALU.mult, ALU.add).then_inc(gamma_parts, 1)
            nc.gpsimd.tensor_scalar(g_neg[:], g_full[:], 1.0, -1.0, ALU.mult, ALU.add).then_inc(gamma_parts, 1)
            pool.wait_ge(stats1_ready, NT)
            pool.wait_ge(gamma_parts, 3)
            step(nc.gpsimd.tensor_scalar(ve[:], mv1[:, :, 1], 1.0, EPS, ALU.mult, ALU.add))
            step(nc.gpsimd.tensor_tensor(rstd[:], ve[:], minus_half[:], ALU.pow))
            nc.gpsimd.tensor_scalar(ln_scale[:], rstd[:], g_rest[:, 0:1], 1.0, ALU.mult, ALU.add).then_inc(ln1_ready, 1)
            step(nc.gpsimd.tensor_tensor(lnb[:], rstd[:], mv1[:, :, 0], ALU.mult))
            nc.gpsimd.tensor_scalar(ln_bias[:], lnb[:], g_neg[:, 0:1], 0.0, ALU.mult, ALU.add).then_inc(ln1_ready, 1)

            def split_lo(slot, uses, i):
                pool.wait_ge(w_hi_ready[slot], len(PIECES) * uses + i + 1)
                nc.gpsimd.tensor_tensor(piece(w_lo[slot], i), piece(raw[slot], i), piece(w_hi[slot], i).bitcast(F32),
                                        ALU.subtract).then_inc((w_lo_gu if i < len(GU_PIECES) else w_lo_d)[slot], 1)

            for i in range(len(PIECES)):
                split_lo(0, 0, i)
            for g in range(NG):
                j = slice(g * TPG, (g + 1) * TPG)
                pool.wait_ge(stats2_ready, TPG * (g + 1))
                step(nc.gpsimd.tensor_scalar(ve2[:, j], mv2[:, j, 1], 1.0, EPS, ALU.mult, ALU.add))
                step(nc.gpsimd.tensor_tensor(rstd2[:, j], ve2[:, j], minus_half[:, j], ALU.pow))
                step(nc.gpsimd.tensor_tensor(nm2[:, j], rstd2[:, j], mv2[:, j, 0], ALU.mult))
                nc.gpsimd.tensor_scalar(nmr2[:, j], nm2[:, j], -1.0, 0.0, ALU.mult, ALU.add).then_inc(ln2_ready, 1)
                if g == NG - 1:
                    pool.dma_start(out_view[:, j, :], x2[:, j, :]).then_inc(landed, 16)
            for g in range(NG):
                pool.wait_ge(hi_ready, g + 1)
                if g:
                    pool.wait_ge(ids_done, g)
                for c in range(2):
                    for r in range(TPG):
                        last = nc.gpsimd.tensor_scalar(id_hi[:, c, r, :], iota_hi[:], hi_f[:, c, r:r + 1],
                                                       id1[:, g * TPG + r:g * TPG + r + 1], ALU.is_equal, ALU.mult)
                last.then_inc(id_hi_ready, 1)

            def gather(t, n, e, tile, slot):
                own_instruction(pool)
                nc.gpsimd.tensor_copy(t.from_rows[slot][:], gather_ids[:, bass.ds(e * MAXT + tile, 1)])\
                  .then_inc(t.from_listed, 1)
                pool.wait_ge(t.from_listed, after(n + 1))
                own_instruction(pool)
                pool.indirect_dma_start(out=t.xg[slot][:], out_offset=None, in_=scratch,
                                        in_offset=bass.IndirectOffsetOnAxis(ap=t.from_rows[slot][:], axis=0))\
                    .then_inc(t.gathered[slot], 16)

            def scatter(t, n, e, tile, scatters_before):
                pool.wait_ge(landed, 16 * (scatters_before + 1))
                own_instruction(pool)
                nc.gpsimd.tensor_copy(t.to_rows[:], scatter_ids[:, bass.ds((e + 1) * MAXT + tile, 1)])\
                  .then_inc(t.to_listed, 1)
                pool.wait_ge(t.to_listed, after(n + 1))
                pool.wait_ge(t.y_ready, after(n + 1))
                own_instruction(pool)
                pool.indirect_dma_start(out=out_rows, in_=t.y[:], in_offset=None,
                                        out_offset=bass.IndirectOffsetOnAxis(ap=t.to_rows[:], axis=0),
                                        bounds_check=TOK - 1, oob_is_err=False, compute_op=ALU.add)\
                    .then_inc(landed, 16)

            pool.wait_ge(lists_ready, 3)
            pool.wait_ge(rows_stored, 16 * NG)
            gather(A, 0, 0, 0, 0)
            gather(Bc, 0, 0, 1, 0)
            first_extras, _ = load_control(pool, 0)
            with pool.If(first_extras > 0):
                gather(C, 0, 0, 2, 0)
            pool.wait_ge(x2_stored, 16 * (NG - 1))
            pool.wait_ge(landed, 16)

            def expert(q, s, last):
                e = 2 * q + s
                extras, so_far = load_control(pool, e)
                if not last:
                    next_extras, next_so_far = load_control(pool, e + 1)
                    gather(A, e + 1, e + 1, 0, 1 - s)
                    pool.wait_ge(Bc.weight_ready, after(e))
                    gather(Bc, e + 1, e + 1, 1, 1 - s)

                def previous_b():
                    split_lo(s, q, 4)
                    scatter(Bc, e - 1, e - 1, 1, 2 * e - 1 + so_far)

                if s == 0:
                    with pool.If(q > 0):
                        previous_b()
                else:
                    previous_b()

                def next_c():
                    with pool.If(next_extras > 0):
                        pool.wait_ge(C.weight_ready, after(next_so_far))
                        gather(C, next_so_far, e + 1, 2, 0)

                if not last:
                    split_lo(1 - s, q + s, 0)
                    with pool.If(extras < 2):
                        next_c()
                scatter(A, e, e, 0, 2 * e + so_far)
                with pool.If(extras > 0):
                    scatter(C, so_far, e, 2, 2 * e + 1 + so_far)
                with pool.If(extras > 1):
                    with pool.Fori(1, extras) as t:
                        n = so_far + t
                        pool.wait_ge(C.weight_ready, after(n))
                        gather(C, n, e, 2 + t, 0)
                        scatter(C, n, e, 2 + t, 2 * e + 1 + n)
                    if not last:
                        next_c()

            with pool.Fori(0, E // 2 - 1) as q:
                expert(q, 0, False)
                expert(q, 1, False)
            expert(E // 2 - 1, 0, False)
            expert(E // 2 - 1, 1, True)
            extras, so_far = load_control(pool, E - 1)
            scatter(Bc, E - 1, E - 1, 1, 2 * E - 1 + so_far + extras)
            pool.wait_ge(landed, 16 * (2 * E + so_far + extras + 1))
            own_instruction(pool)


def kernel(**inputs):
    import numpy as np
    import concourse.bacc as bacc
    from concourse import mybir as my
    from concourse.bass_utils import run_bass_kernel_spmd as run

    a = {k: np.asarray(v) for k, v in inputs.items()}
    e, f, h = a["L0_ffn_gate_w"].shape
    kc = h // 128
    whole = f // 128 * 128
    down_t = a["L0_ffn_down_w"].transpose(0, 2, 1)

    def contraction_first(w):
        return w.reshape(e, f, kc, 128).transpose(0, 3, 2, 1).reshape(e, 128, kc * f)

    laid_out = {
        "x": a["x"],
        "ctxT": a["ctx_512"].reshape(-1, a["ctx_512"].shape[-1]).T,
        "wq": a["L0_xattn_Wq"],
        "wk": a["L0_xattn_Wk"],
        "gamma": a["L0_xattn_gamma_raw"].reshape(1),
        "routerT": a["L0_ffn_router_w"].reshape(e, kc, 128).transpose(2, 1, 0),
        "gate": contraction_first(a["L0_ffn_gate_w"]),
        "up": contraction_first(a["L0_ffn_up_w"]),
        "down": down_t[:, :whole].reshape(e, whole // 128, 128, h).transpose(0, 2, 1, 3).reshape(e, 128, -1),
        "down_rest": down_t[:, whole:],
    }
    nc = bacc.Bacc("TRN2", target_bir_lowering=False, num_devices=1)
    arrays, args = {}, []
    for name, v in laid_out.items():
        v = np.ascontiguousarray(v)
        arrays[f"in_{name}"] = v
        args.append(nc.dram_tensor(f"in_{name}", v.shape, my.dt.from_np(v.dtype), kind="ExternalInput").ap())
    args.append(nc.dram_tensor("out_0", a["x"].shape, my.dt.from_np(a["x"].dtype), kind="ExternalOutput").ap())
    xattn_moe_kernel(nc, *args)
    return run(nc, [arrays], core_ids=[0]).results[0]["out_0"]
```

```python
import concourse.bass as bass
from concourse import mybir
from contextlib import ExitStack

F32 = mybir.dt.float32
F32R = mybir.dt.float32r
F16 = mybir.dt.float16
I32 = mybir.dt.int32
U32 = mybir.dt.uint32
ALU = mybir.AluOpType
ACT = mybir.ActivationFunctionType
AX = mybir.AxisListType

P = 128
B, N, D = 4, 256, 64
H = 256
TOK = B * N
NT = TOK // P
TPB = N // P
BPG = 2
NG = B // BPG
TPG = BPG * TPB
KTOP = int(N * 0.3)
ROUNDS = (KTOP + 7) // 8
E, F = 8, 688
KC = H // P
FCH = F // 2
FB = (F + P - 1) // P
FREST = F - (FB - 1) * P
REST2 = P // 2
GU_COLS = 2 * KC * F
W_COLS = GU_COLS + FB * H
MAXT = TOK // P
LOG_MAXT = MAXT.bit_length() - 1
EPS = 1e-5
LOWEST = -3.4e38
STEPS_OF_GUESS = 3
GUESS_DENSITY = 130.0
WINDOW = 16
COUNT_MID = KTOP - (WINDOW + 1) / 2
TARGET = KTOP - WINDOW // 2
SKIP = 4096.0
ROW = H + E

GU_PIECES = [(i * F, F) for i in range(2 * KC)]
D_PIECES = [(GU_COLS + i * (FB * H // 2), FB * H // 2) for i in range(2)]
PIECES = GU_PIECES + D_PIECES

SIM = [0, 1, 2, 3]
PROJ = [4, 5, 6, 7]
XNT, LOG, IDS = [4, 5], [6, 0], 7
RANK_AT = TPG * E
COUNT_AT = 2 * TPG * E
GB, UB = [0, 2], [1, 3]
TB = [4, 6]
XB, YB = 5, 7


def after(tiles):
    return tiles + 1


class TileClass:

    def __init__(self, name, sb, sem, gather_slots):
        self.name = name
        self.xg = [sb(f"xg{name}{i}", [P, ROW], F32) for i in range(gather_slots)]
        self.xt_hi = sb(f"xt_hi{name}", [P, KC, P], F32R)
        self.xt_lo = sb(f"xt_lo{name}", [P, KC, P], F32R)
        self.h = sb(f"h{name}", [P, FB * P], F32)
        self.y = sb(f"y{name}", [P, H], F32)
        self.weight = [sb(f"weight{name}{i}", [P, 1], F32) for i in range(gather_slots)]
        self.from_rows = [sb(f"from_rows{name}{i}", [P, 1], U32) for i in range(gather_slots)]
        self.to_rows = sb(f"to_rows{name}", [P, 1], U32)
        self.gathered = [sem(f"gathered{name}{i}") for i in range(gather_slots)]
        self.from_listed = sem(f"from_listed{name}")
        self.to_listed = sem(f"to_listed{name}")
        self.x_transposed = sem(f"x_transposed{name}")
        self.x_hi_ready = sem(f"x_hi_ready{name}")
        self.x_ready = sem(f"x_ready{name}")
        self.weight_ready = sem(f"weight_ready{name}")
        self.gu_done = [sem(f"gu_done{name}{c}") for c in range(2)]
        self.silu_ready = [sem(f"silu_ready{name}{c}") for c in range(2)]
        self.h_ready = [sem(f"h_ready{name}{c}") for c in range(2)]
        self.h_transposed = [sem(f"h_transposed{name}{c}") for c in range(2)]
        self.ht_hi_ready = [sem(f"ht_hi_ready{name}{c}") for c in range(2)]
        self.ht_ready = [sem(f"ht_ready{name}{c}") for c in range(2)]
        self.down_done = sem(f"down_done{name}")
        self.y_ready = sem(f"y_ready{name}")

    def start_counts(self, eng):
        for s in (self.from_listed, self.to_listed, self.x_transposed, self.x_hi_ready, self.x_ready, self.weight_ready,
                  *self.gu_done,
                  *self.silu_ready, *self.h_ready, *self.h_transposed, *self.ht_hi_ready, *self.ht_ready,
                  self.down_done, self.y_ready):
            eng.sem_inc(s, 1)


assert STEPS_OF_GUESS == 3 and B == 4


def xattn_moe_kernel(nc, x, ctxT, wq, wk, gamma, routerT, gate, up, down, down_rest, out):
    scratch = nc.dram_tensor("xn_rows", (TOK, ROW), F32, kind="Internal").ap()
    x_view = x.rearrange("b (r p) d -> p (b r) d", p=P)
    out_view = out.rearrange("b (r p) d -> p (b r) d", p=P)
    out_rows = out.rearrange("b n d -> (b n) d")
    scratch_view = scratch.rearrange("(j p) d -> p j d", p=P)

    ctx = ExitStack()
    with ctx:
        def sb(name, shape, dt):
            return ctx.enter_context(nc.sbuf_tensor(name, shape, dt))

        def sem(name):
            return ctx.enter_context(nc.semaphore(name))

        ps = ctx.enter_context(nc.psum_tensor("ps", [P, 8, 512], F32))

        xs = sb("xs", [P, NT, H], F32)
        x2 = sb("x2", [P, NT, H], F32)
        xn = sb("xn", [P, NT, ROW], F32)
        ctx_sb = sb("ctx_sb", [D, TOK], F32)
        wq_sb = sb("wq_sb", [D, D], F32)
        wk_sb = sb("wk_sb", [D, D], F32)
        m_sb = sb("m_sb", [D, D], F32)
        mT = sb("mT", [D, TOK], F32)
        sim = sb("sim", [P, NT, N], F32)
        att = sb("att", [P, NT, N], F32)
        work = sb("work", [P, TPB, N], F32)
        top = sb("top", [P, NT, WINDOW], F32)
        mvs = sb("mvs", [P, NT, 2], F32)
        deviation = sb("deviation", [P, NT], F32)
        move = sb("move", [P, NT], F32)
        guess = sb("guess", [P, NT], F32)
        guess_base = sb("guess_base", [P, NT], F32)
        slope = sb("slope", [P, NT], F32)
        slope_base = sb("slope_base", [P, NT], F32)
        half = sb("half", [P, NT], F32)
        signs = sb("signs", [P, NT], F32)
        above = sb("above", [P, NT], F32)
        wanted = sb("wanted", [P, NT], F32)
        chosen = sb("chosen", [P, NT, WINDOW], F32)
        threshold = sb("threshold", [P, NT], F32)
        off = sb("off", [P, NT], F32)
        off_squared = sb("off_squared", [P, NT], F32)
        missed = sb("missed", [P, NT], F32)
        missed_sum = sb("missed_sum", [P, 1], F32)
        missed_any = sb("missed_any", [P, 1], I32)
        work1 = sb("work1", [P, N], F32)
        top1 = sb("top1", [P, 8], F32)
        xnT = sb("xnT", [P, TPG, KC, P], F32)
        rw = sb("rw", [P, KC, E], F32)
        gam = sb("gam", [P, 1], F32)
        g_full = sb("g_full", [P, 1], F32)
        g_half = sb("g_half", [P, 1], F32)
        g_rest = sb("g_rest", [P, 1], F32)
        g_neg = sb("g_neg", [P, 1], F32)
        stats = sb("stats", [P, NT, 6], F32)
        stats_sim = sb("stats_sim", [P, NT, 6], F32)
        mv1 = sb("mv1", [P, NT, 2], F32)
        mv2 = sb("mv2", [P, NT, 2], F32)
        ve = sb("ve", [P, NT], F32)
        rstd = sb("rstd", [P, NT], F32)
        lnb = sb("lnb", [P, NT], F32)
        lna = sb("lna", [P, NT], F32)
        ln_scale = sb("ln_scale", [P, NT], F32)
        ln_bias = sb("ln_bias", [P, NT], F32)
        ve2 = sb("ve2", [P, NT], F32)
        rstd2 = sb("rstd2", [P, NT], F32)
        nm2 = sb("nm2", [P, NT], F32)
        nmr2 = sb("nmr2", [P, NT], F32)
        minus_half = sb("minus_half", [P, NT], F32)
        ident = sb("ident", [P, P], F32)
        ones_f = sb("ones_f", [P, P], F32)
        earlier = sb("earlier", [P, P], F16)
        ones_h = sb("ones_h", [P, P], F16)
        iota_e = sb("iota_e", [P, E], F32)
        iota_lo = sb("iota_lo", [P, P], F16)
        iota_hi = sb("iota_hi", [P, E * MAXT], F16)
        id1 = sb("id1", [P, NT], F32)
        lim = sb("lim", [P, MAXT], F32)
        lmax = sb("lmax", [P, NT, 8], F32)
        lidx = sb("lidx", [P, NT, 8], U32)
        diff = sb("diff", [P, NT], F32)
        prob = sb("prob", [P, 2, NT], F32)
        onehot = sb("onehot", [P, NG, 2, TPG, E], F32)
        picked = sb("picked", [P, NT, E], F16)
        wsel = sb("wsel", [P, 2, TPG, E], F32)
        rsel = sb("rsel", [P, 2, TPG, E], F32)
        rank = sb("rank", [P, 2, TPG], F32)
        rank_i = sb("rank_i", [P, 2, TPG], I32)
        lo_i = sb("lo_i", [P, 2, TPG], I32)
        hi_i = sb("hi_i", [P, 2, TPG], I32)
        lo_f = sb("lo_f", [P, 2, TPG], F32)
        hi_f = sb("hi_f", [P, 2, TPG], F32)
        oh_lo = sb("oh_lo", [P, 2, TPG, P], F16)
        oh_hi = sb("oh_hi", [P, 2, TPG, E * MAXT], F16)
        id_hi = sb("id_hi", [P, 2, TPG, E * MAXT], F16)
        idm = sb("idm", [P, E * MAXT], F32)
        pad = sb("pad", [P, E * MAXT], F32)
        gather_ids = sb("gather_ids", [P, E * MAXT + 1], U32)
        scatter_ids = sb("scatter_ids", [P, MAXT + E * MAXT + 1], U32)
        counts = sb("counts", [P, E], F32)
        over = sb("over", [P, E, MAXT - 2], F32)
        extra = sb("extra", [P, E], F32)
        extra_before = sb("extra_before", [P, 2, E], F32)
        control = sb("control", [P, E], F32)
        ctl = sb("ctl", [P, E], I32)
        raw = [sb(f"raw{i}", [P, W_COLS], F32) for i in range(2)]
        w_hi = [sb(f"w_hi{i}", [P, W_COLS], F32R) for i in range(2)]
        w_lo = [sb(f"w_lo{i}", [P, W_COLS - H], F32R) for i in range(2)]
        silu = [sb(f"silu{c}", [P, FCH], F32) for c in range(2)]
        ht_hi = sb("ht_hi", [P, FB, P], F32R)
        ht_lo = sb("ht_lo", [P, FB, P], F32R)

        A = TileClass("A", sb, sem, 2)
        Bc = TileClass("B", sb, sem, 2)
        C = TileClass("C", sb, sem, 1)

        x_loaded, ctx_loaded, small_loaded = sem("x_loaded"), sem("ctx_loaded"), sem("small_loaded")
        raw_loaded = [sem(f"raw_loaded{i}") for i in range(2)]
        w_hi_ready = [sem(f"w_hi_ready{i}") for i in range(2)]
        w_lo_gu = [sem(f"w_lo_gu{i}") for i in range(2)]
        w_lo_d = [sem(f"w_lo_d{i}") for i in range(2)]
        const_step, const_ready = sem("const_step"), sem("const_ready")
        cleared = sem("cleared")
        waits_passed = sem("waits_passed")
        m_done, m_ready = sem("m_done"), sem("m_ready")
        proj_done, proj_ready = sem("proj_done"), sem("proj_ready")
        sim_done, sim_copied, sig_ready = sem("sim_done"), sem("sim_copied"), sem("sig_ready")
        sim_stats = sem("sim_stats")
        guess_ready = [sem(f"guess_ready{b}") for b in range(B)]
        signs_counted = sem("signs_counted")
        missed_ready, missed_done, general_step = sem("missed_ready"), sem("missed_done"), sem("general_step")
        missed_seen, x2_summed = sem("missed_seen"), sem("x2_summed")
        gamma_ready, gamma_parts = sem("gamma_ready"), sem("gamma_parts")
        stats1_ready, ln1_ready, base_ready = sem("stats1_ready"), sem("ln1_ready"), sem("base_ready")
        pool_step, dve_step = sem("pool_step"), sem("dve_step")
        att_ready, sum_done, x2_ready = sem("att_ready"), sem("sum_done"), sem("x2_ready")
        stats2_ready, ln2_ready, xn_ready = sem("stats2_ready"), sem("ln2_ready"), sem("xn_ready")
        xnt_done, xnt_ready, logits_done = sem("xnt_done"), sem("xnt_ready"), sem("logits_done")
        rstd2_ready, xn_ready_last = sem("rstd2_ready"), sem("xn_ready_last")
        diff_ready, prob_ready, row_ready = sem("diff_ready"), sem("prob_ready"), sem("row_ready")
        picked_ready, rank_done, one_hots_ready = sem("picked_ready"), sem("rank_done"), sem("one_hots_ready")
        ids_done, lists_ready = sem("ids_done"), sem("lists_ready")
        gather_listed = sem("gather_listed")
        x2_stored, rows_stored = sem("x2_stored"), sem("rows_stored")
        landed = sem("landed")

        block = ctx.enter_context(nc.Block())

        def piece(w, i):
            return w[:, PIECES[i][0]:PIECES[i][0] + PIECES[i][1]]

        def split_low(ns, slot, i):
            c0, c1 = PIECES[i][0], min(PIECES[i][0] + PIECES[i][1], W_COLS - H)
            return ns.tensor_tensor(w_lo[slot][:, c0:c1], raw[slot][:, c0:c1], w_hi[slot][:, c0:c1].bitcast(F32),
                                    ALU.subtract)

        def split_low_rest(ns, slot):
            rows, cols = slice(REST2, REST2 + FREST), slice(W_COLS - H, W_COLS)
            return ns.tensor_tensor(w_hi[slot][rows, cols], raw[slot][rows, cols], w_hi[slot][rows, cols].bitcast(F32),
                                    ALU.subtract)

        passes = [(0, 0), (0, 1), (1, 0), (0, 2), (1, 1), (1, 2), (2, 0), (3, 0), (2, 1), (3, 1), (2, 2), (3, 2)]

        def own_instruction(eng):
            eng.sem_inc(waits_passed, 1)

        def load_control(eng, e):
            at = slice(e, e + 1) if isinstance(e, int) else bass.ds(e, 1)
            packed = eng.value_load(ctl[0:1, at], min_val=0, max_val=MAXT * (2 * TOK // P) + MAXT - 2)
            return packed & (MAXT - 1), packed >> LOG_MAXT

        @block.sync
        def _(sp):
            def load_expert(e, slot):
                sp.dma_start(raw[slot][:, 0:KC * F], gate[e]).then_inc(raw_loaded[slot], 16)
                sp.dma_start(raw[slot][:, KC * F:GU_COLS], up[e]).then_inc(raw_loaded[slot], 16)
                sp.dma_start(raw[slot][:, GU_COLS:W_COLS - H], down[e]).then_inc(raw_loaded[slot], 16)
                for row in (0, REST2):
                    sp.dma_start(raw[slot][row:row + FREST, W_COLS - H:W_COLS], down_rest[e])\
                      .then_inc(raw_loaded[slot], 16)

            sp.dma_start(wq_sb[:], wq).then_inc(ctx_loaded, 16)
            sp.dma_start(wk_sb[:], wk).then_inc(ctx_loaded, 16)
            sp.dma_start(ctx_sb[:], ctxT).then_inc(ctx_loaded, 16)
            sp.dma_start(xs[:], x_view).then_inc(x_loaded, 16)
            sp.dma_start(gam[:], gamma.partition_broadcast(P)).then_inc(small_loaded, 16)
            sp.dma_start(rw[:], routerT).then_inc(small_loaded, 16)
            sp.wait_ge(cleared, 2)
            load_expert(0, 0)
            load_expert(1, 1)
            for t in (A, Bc, C):
                t.start_counts(sp)
            for g in range(NG):
                j = slice(g * TPG, (g + 1) * TPG)
                if g < NG - 1:
                    sp.wait_ge(x2_ready, BPG * (g + 1))
                    sp.dma_start(out_view[:, j, :], x2[:, j, :]).then_inc(x2_stored, 16)
                sp.wait_ge(row_ready, g + 1)
                sp.dma_start(scratch_view[:, j, :], xn[:, j, :]).then_inc(rows_stored, 16)
            sp.wait_ge(A.gathered[0], 16)
            sp.wait_ge(Bc.gathered[0], 16)
            with sp.Fori(0, E // 2 - 1) as q:
                for s in range(2):
                    sp.wait_ge(w_lo_gu[s], 4 * q + 4)
                    sp.wait_ge(w_lo_d[s], 2 * q + 2)
                    e = 2 * q + s + 2
                    for dst, src in ((raw[s][:, 0:KC * F], gate), (raw[s][:, KC * F:GU_COLS], up),
                                     (raw[s][:, GU_COLS:W_COLS - H], down),
                                     (raw[s][0:FREST, W_COLS - H:W_COLS], down_rest),
                                     (raw[s][REST2:REST2 + FREST, W_COLS - H:W_COLS], down_rest)):
                        sp.dma_start(dst, src[bass.ds(e, 1)].rearrange("a p c -> p (a c)"))\
                          .then_inc(raw_loaded[s], 16)

        @block.tensor
        def _(pe):
            def keep_clock_up(products, bank):
                for _ in range(products):
                    nc.tensor.matmul(ps[:, bank, 0:P], ones_f[:], ones_f[:], start=True, stop=True)

            def project(b):
                nc.tensor.matmul(ps[0:D, PROJ[b], 0:N], m_sb[:], ctx_sb[:, b * N:(b + 1) * N],
                                 start=True, stop=True).then_inc(proj_done, 1)

            def similarities(b):
                pe.wait_ge(proj_ready, b + 1)
                for r in range(TPB):
                    j = b * TPB + r
                    nc.tensor.matmul(ps[:, SIM[b], r * N:(r + 1) * N], mT[:, j * P:(j + 1) * P],
                                     ctx_sb[:, b * N:(b + 1) * N], start=True, stop=True).then_inc(sim_done, 1)

            pe.wait_ge(const_step, 1)
            keep_clock_up(11, IDS)
            pe.wait_ge(ctx_loaded, 48)
            nc.tensor.matmul(ps[0:D, PROJ[0], N:N + D], wq_sb[:], wk_sb[:], start=True, stop=True).then_inc(m_done, 1)
            pe.wait_ge(m_ready, 1)
            project(0)
            for b in range(B):
                if b < B - 1:
                    project(b + 1)
                similarities(b)
            pe.wait_ge(const_ready, 1)
            pe.wait_ge(small_loaded, 32)
            pe.wait_ge(missed_ready, 1)
            nc.tensor.matmul(ps[:, IDS, 0:1], ones_f[:], missed_sum[:], start=True, stop=True).then_inc(missed_done, 1)

            def symmetrise(b):
                pe.wait_ge(att_ready, TPB * (b + 1))
                for r in range(TPB):
                    nc.tensor.matmul(ps[:, SIM[b], r * N:(r + 1) * N], ident[:], att[:, b * TPB + r, :],
                                     start=True, stop=False)
                    for c in range(TPB):
                        last = nc.tensor.matmul(ps[:, SIM[b], r * N + c * P:r * N + (c + 1) * P],
                                                att[:, b * TPB + c, r * P:(r + 1) * P], ident[:],
                                                start=False, stop=(c == TPB - 1))
                last.then_inc(sum_done, 1)

            def transpose_normalised(g):
                if g:
                    pe.wait_ge(xnt_ready, BPG * g)
                for b in range(BPG):
                    if g < NG - 1:
                        pe.wait_ge(xn_ready, g * TPG + TPB * (b + 1))
                    else:
                        pe.wait_ge(xn_ready_last, TPB * (b + 1))
                    for r in range(TPB):
                        for k in range(KC):
                            last = nc.tensor.transpose(ps[:, XNT[b], (r * KC + k) * P:(r * KC + k + 1) * P],
                                                       xn[:, g * TPG + b * TPB + r, k * P:(k + 1) * P], ident[:])
                    last.then_inc(xnt_done, 1)

            def logits(g):
                for b in range(BPG):
                    pe.wait_ge(xnt_ready, BPG * g + b + 1)
                    for r in range(b * TPB, (b + 1) * TPB):
                        for k in range(KC):
                            last = nc.tensor.matmul(ps[:, LOG[g], r * E:(r + 1) * E], xnT[:, r, k, :], rw[:, k, :],
                                                    start=(k == 0), stop=(k == KC - 1))
                last.then_inc(logits_done, 1)

            def ranks(g):
                pe.wait_ge(picked_ready, g + 1)
                if g == NG - 1:
                    for t in range(NT):
                        nc.tensor.matmul(ps[:, LOG[g], COUNT_AT:COUNT_AT + E], ones_h[:], picked[:, t, :],
                                         start=(t == 0), stop=(t == NT - 1))
                first = g * TPG
                nc.tensor.matmul(ps[:, LOG[g], RANK_AT:RANK_AT + TPG * E], earlier[:],
                                 picked[:, first:first + TPG, :].rearrange("p j e -> p (j e)"), start=True, stop=False)
                for t in range(first + TPG - 1):
                    r = max(t + 1, first) - first
                    last = nc.tensor.matmul(ps[:, LOG[g], RANK_AT + r * E:RANK_AT + TPG * E], ones_h[:],
                                            picked[:, t:t + 1, :].to_broadcast([P, TPG - r, E]),
                                            start=False, stop=(t == first + TPG - 2))
                last.then_inc(rank_done, 1)

            def token_ids(g):
                pe.wait_ge(one_hots_ready, g + 1)
                for c in range(2):
                    for r in range(TPG):
                        last = nc.tensor.matmul(ps[:, IDS, 0:E * MAXT], oh_lo[:, c, r, :], id_hi[:, c, r, :],
                                                start=(g == 0 and c == 0 and r == 0),
                                                stop=(g == NG - 1 and c == 1 and r == TPG - 1))
                last.then_inc(ids_done, 1)

            keep_clock_up(6, XNT[0])
            for b in range(B):
                symmetrise(b)
            pe.wait_ge(missed_seen, 1)
            keep_clock_up(8, IDS)
            transpose_normalised(0)
            logits(0)
            for g in range(NG):
                if g < NG - 1:
                    transpose_normalised(g + 1)
                ranks(g)
                if g < NG - 1:
                    logits(g + 1)
                token_ids(g)

            def x_transpose(t, n, slot, gathers):
                pe.wait_ge(t.gathered[slot], 16 * gathers)
                for k in range(KC):
                    last = nc.tensor.transpose(ps[:, XB, k * P:(k + 1) * P], t.xg[slot][:, k * P:(k + 1) * P], ident[:])
                last.then_inc(t.x_transposed, 1)

            def gate_up(t, n, c, s):
                if c == 0:
                    pe.wait_ge(t.x_ready, after(n + 1))
                for bank, m in ((GB[c], 0), (UB[c], 1)):
                    for k in range(KC):
                        lo = (m * KC + k) * F + c * FCH
                        hi_w, lo_w = w_hi[s][:, lo:lo + FCH], w_lo[s][:, lo:lo + FCH]
                        o = ps[:, bank, 0:FCH]
                        nc.tensor.matmul(o, t.xt_hi[:, k, :], hi_w, start=(k == 0), stop=False)
                        nc.tensor.matmul(o, t.xt_hi[:, k, :], lo_w, start=False, stop=False)
                        last = nc.tensor.matmul(o, t.xt_lo[:, k, :], hi_w, start=False, stop=(k == KC - 1))
                last.then_inc(t.gu_done[c], 1)

            def h_transpose(t, n):
                for i, blocks in enumerate((range(0, 4), range(4, FB))):
                    pe.wait_ge(t.h_ready[1 - i], after(n + 1))
                    for f in blocks:
                        last = nc.tensor.transpose(ps[:, TB[i], (f % 4) * P:(f % 4 + 1) * P],
                                                   t.h[:, f * P:(f + 1) * P], ident[:])
                    last.then_inc(t.h_transposed[i], 1)

            def down_product(t, n, s):
                o = ps[:, YB, 0:H]
                for f in range(FB):
                    if f == 0:
                        pe.wait_ge(t.ht_ready[0], after(n + 1))
                    if f == 4:
                        pe.wait_ge(t.ht_ready[1], after(n + 1))
                    lo = GU_COLS + f * H
                    hi_w = w_hi[s][:, lo:lo + H]
                    nc.tensor.matmul(o, ht_hi[:, f, :], hi_w, start=(f == 0), stop=False)
                    if f < FB - 1:
                        nc.tensor.matmul(o, ht_hi[:, f, :], w_lo[s][:, lo:lo + H], start=False, stop=False)
                    last = nc.tensor.matmul(o, ht_lo[:, f, :], hi_w, start=False, stop=(f == FB - 1))
                last.then_inc(t.down_done, 1)

            def expert(q, s, last):
                e = 2 * q + s
                extras, so_far = load_control(pe, e)
                pe.wait_ge(w_lo_gu[s], 4 * q + 4)

                def previous_b_transpose():
                    h_transpose(Bc, e - 1)

                def previous_b_down():
                    pe.wait_ge(A.y_ready, after(e))
                    pe.wait_ge(C.y_ready, after(so_far))
                    down_product(Bc, e - 1, 1 - s)

                pe.wait_ge(Bc.h_ready[0], after(e))
                gate_up(A, e, 0, s)
                x_transpose(Bc, e, s, q + 1)
                if s == 0:
                    with pe.If(q > 0):
                        previous_b_transpose()
                else:
                    previous_b_transpose()
                pe.wait_ge(Bc.h_ready[1], after(e))
                gate_up(A, e, 1, s)

                def b_down():
                    if s == 0:
                        with pe.If(q > 0):
                            previous_b_down()
                    else:
                        previous_b_down()

                def next_a():
                    if not last:
                        pe.wait_ge(Bc.x_ready, after(e + 1))
                        x_transpose(A, e + 1, 1 - s, q + 1 + s)

                with pe.If(extras > 0):
                    n = so_far
                    pe.wait_ge(Bc.x_ready, after(e + 1))
                    x_transpose(C, n, 0, n + 1)
                    b_down()
                    h_transpose(A, e)
                    gate_up(C, n, 0, s)
                    pe.wait_ge(Bc.y_ready, after(e))
                    pe.wait_ge(w_lo_d[s], 2 * q + 2)
                    down_product(A, e, s)
                    gate_up(C, n, 1, s)
                    next_a()
                    pe.wait_ge(C.h_ready[0], after(n + 1))
                    gate_up(Bc, e, 0, s)
                    h_transpose(C, n)
                    gate_up(Bc, e, 1, s)
                    pe.wait_ge(A.y_ready, after(e + 1))
                    down_product(C, n, s)
                    if not last:
                        pe.wait_ge(A.x_ready, after(e + 2))
                    with pe.If(extras > 1):
                        pe.wait_ge(Bc.h_ready[0], after(e + 1))
                        pe.wait_ge(Bc.h_ready[1], after(e + 1))
                        own_instruction(pe)
                        with pe.Fori(1, extras) as t:
                            n = so_far + t
                            pe.wait_ge(C.y_ready, after(n))
                            x_transpose(C, n, 0, n + 1)
                            gate_up(C, n, 0, s)
                            gate_up(C, n, 1, s)
                            h_transpose(C, n)
                            down_product(C, n, s)
                with pe.Else():
                    b_down()
                    h_transpose(A, e)
                    next_a()
                    gate_up(Bc, e, 0, s)
                    if last:
                        gate_up(Bc, e, 1, s)
                    pe.wait_ge(Bc.y_ready, after(e))
                    pe.wait_ge(w_lo_d[s], 2 * q + 2)
                    down_product(A, e, s)
                    if not last:
                        gate_up(Bc, e, 1, s)

            keep_clock_up(10, GB[1])
            pe.wait_ge(xnt_ready, B)
            x_transpose(A, 0, 0, 1)
            pe.wait_ge(lists_ready, 2)
            with pe.Fori(0, E // 2 - 1) as q:
                expert(q, 0, False)
                expert(q, 1, False)
            expert(E // 2 - 1, 0, False)
            expert(E // 2 - 1, 1, True)
            h_transpose(Bc, E - 1)
            extras, so_far = load_control(pe, E - 1)
            pe.wait_ge(A.y_ready, after(E))
            pe.wait_ge(C.y_ready, after(so_far + extras))
            down_product(Bc, E - 1, 1)

        @block.scalar
        def _(act):
            def copy_sim(b):
                act.wait_ge(sim_done, TPB * (b + 1))
                j = slice(b * TPB, (b + 1) * TPB)
                nc.scalar.copy(sim[:, j, :], ps[:, SIM[b], :].rearrange("p (r n) -> p r n", r=TPB))\
                  .then_inc(sim_copied, 1)

            copy_sim(0)
            copy_sim(1)
            for at, (b, i) in enumerate(passes):
                if at in (1, 2):
                    copy_sim(at + 1)
                act.wait_ge(guess_ready[b], i + 1)
                for r in range(TPB):
                    j = b * TPB + r
                    nc.scalar.activation(att[:, j, :], sim[:, j, :], ACT.Sign, scale=-1.0, bias=guess[:, j:j + 1],
                                         accum_out=signs[:, j:j + 1]).then_inc(signs_counted, 1)
            act.wait_ge(small_loaded, 32)
            nc.scalar.activation(g_full[:], gam[:], ACT.Sigmoid).then_inc(gamma_ready, 1)
            act.wait_ge(signs_counted, TPB * len(passes))
            for b in range(B):
                j = slice(b * TPB, (b + 1) * TPB)
                nc.scalar.activation(att[:, j, :], sim[:, j, :], ACT.Sigmoid).then_inc(sig_ready, 1)
            act.wait_ge(raw_loaded[0], 80)
            for i in range(len(PIECES)):
                nc.scalar.activation(piece(w_hi[0], i), piece(raw[0], i), ACT.Copy).then_inc(w_hi_ready[0], 1)
            act.wait_ge(ln1_ready, 2)
            for j in range(NT):
                nc.scalar.activation(xs[:, j, :], xs[:, j, :], ACT.Identity, scale=ln_scale[:, j:j + 1],
                                     bias=ln_bias[:, j:j + 1]).then_inc(base_ready, 1)

            def normalise(g):
                act.wait_ge(ln2_ready, g + 1)
                for j in range(g * TPG, (g + 1) * TPG):
                    nc.scalar.activation(xn[:, j, 0:H], x2[:, j, :], ACT.Identity, scale=rstd2[:, j:j + 1],
                                         bias=nmr2[:, j:j + 1]).then_inc(xn_ready, 1)

            normalise(0)
            for g in range(NG):
                if g:
                    act.wait_ge(logits_done, g)
                for b in range(BPG):
                    act.wait_ge(xnt_done, BPG * g + b + 1)
                    nc.scalar.activation(xnT[:, b * TPB:(b + 1) * TPB],
                                         ps[:, XNT[b], :].rearrange("p (r k t) -> p r k t", r=TPB, k=KC), ACT.Copy)\
                      .then_inc(xnt_ready, 1)
                if g < NG - 2:
                    normalise(g + 1)
                act.wait_ge(diff_ready, g + 1)
                j = slice(g * TPG, (g + 1) * TPG)
                nc.scalar.activation(prob[:, 0, j], diff[:, j], ACT.Sigmoid).then_inc(prob_ready, 1)
                nc.scalar.activation(prob[:, 1, j], diff[:, j], ACT.Sigmoid, scale=-1.0).then_inc(prob_ready, 1)

            def x_hi(t, n):
                act.wait_ge(t.x_transposed, after(n + 1))
                nc.scalar.copy(t.xt_hi[:], ps[:, XB, 0:H].rearrange("p (k t) -> p k t", k=KC))\
                  .then_inc(t.x_hi_ready, 1)

            def gate_silu(t, n, c):
                act.wait_ge(t.gu_done[c], after(n + 1))
                nc.scalar.activation(silu[c][:], ps[:, GB[c], 0:FCH], ACT.Silu).then_inc(t.silu_ready[c], 1)

            def ht_high(t, n):
                for i, (f0, f1) in enumerate(((0, 4), (4, FB))):
                    act.wait_ge(t.h_transposed[i], after(n + 1))
                    nc.scalar.copy(ht_hi[:, f0:f1, :],
                                   ps[:, TB[i], 0:(f1 - f0) * P].rearrange("p (f t) -> p f t", t=P)).then_inc(t.ht_hi_ready[i], 1)

            def expert(q, s, last):
                e = 2 * q + s
                extras, so_far = load_control(act, e)

                def split_next(*pieces):
                    if last:
                        return
                    for i in pieces:
                        if i == 0:
                            act.wait_ge(raw_loaded[1 - s], 80 * (q + s + 1))
                            act.wait_ge(Bc.gu_done[1], after(e))
                            act.wait_ge(C.gu_done[1], after(so_far))
                        if i == len(GU_PIECES):
                            act.wait_ge(Bc.down_done, after(e))
                            act.wait_ge(C.down_done, after(so_far))
                        nc.scalar.copy(piece(w_hi[1 - s], i), piece(raw[1 - s], i))\
                          .then_inc(w_hi_ready[1 - s], 1)

                gate_silu(A, e, 0)
                x_hi(Bc, e)
                if s == 0:
                    with act.If(q > 0):
                        ht_high(Bc, e - 1)
                else:
                    ht_high(Bc, e - 1)
                split_next(0)
                gate_silu(A, e, 1)
                split_next(1)
                with act.If(extras > 0):
                    n = so_far
                    x_hi(C, n)
                    ht_high(A, e)
                    gate_silu(C, n, 0)
                    split_next(2)
                    gate_silu(C, n, 1)
                    if not last:
                        x_hi(A, e + 1)
                    split_next(3)
                    gate_silu(Bc, e, 0)
                    ht_high(C, n)
                with act.Else():
                    ht_high(A, e)
                    if not last:
                        x_hi(A, e + 1)
                    split_next(2)
                    gate_silu(Bc, e, 0)
                    split_next(3)
                split_next(4)
                gate_silu(Bc, e, 1)
                split_next(5)
                with act.If(extras > 1):
                    with act.Fori(1, extras) as t:
                        n = so_far + t
                        x_hi(C, n)
                        gate_silu(C, n, 0)
                        gate_silu(C, n, 1)
                        ht_high(C, n)

            nc.scalar.preload_act_table(ACT.Silu)
            act.wait_ge(lists_ready, 2)
            x_hi(A, 0)
            with act.Fori(0, E // 2 - 1) as q:
                expert(q, 0, False)
                expert(q, 1, False)
            expert(E // 2 - 1, 0, False)
            expert(E // 2 - 1, 1, True)
            ht_high(Bc, E - 1)

        @block.vector
        def _(dve):
            steps = [0]

            def step(ins):
                steps[0] += 1
                ins.then_inc(dve_step, 1)
                dve.wait_ge(dve_step, steps[0])

            for s in range(2):
                nc.vector.memset(raw[s][:, W_COLS - H:W_COLS], 0.0).then_inc(cleared, 1)
            for t in (A, Bc, C):
                nc.vector.memset(t.h[:, F:FB * P], 0.0).then_inc(cleared, 1)

            def projected(b):
                dve.wait_ge(proj_done, b + 1)
                nc.vector.tensor_scalar(mT[:, b * N:(b + 1) * N], ps[0:D, PROJ[b], 0:N], 1.0 / 16.0, None, ALU.mult)\
                  .then_inc(proj_ready, 1)

            def sim_statistics(b):
                dve.wait_ge(sim_copied, b + 1)
                for r in range(TPB):
                    nc.vector.bn_stats(stats_sim[:, b * TPB + r, :], sim[:, b * TPB + r, :]).then_inc(dve_step, 1)
                steps[0] += TPB
                dve.wait_ge(dve_step, steps[0])
                for r in range(TPB):
                    nc.vector.bn_aggr(mvs[:, b * TPB + r, :], stats_sim[:, b * TPB + r, :]).then_inc(sim_stats, 1)

            def both(*makers):
                done = [0] * TPB
                for make in makers:
                    for r in range(TPB):
                        if done[r]:
                            dve.wait_ge(dve_step, done[r])
                        make(r).then_inc(dve_step, 1)
                        steps[0] += 1
                        done[r] = steps[0]
                dve.wait_ge(dve_step, steps[0])

            def find_threshold(b):
                t = b * TPB
                dve.wait_ge(guess_ready[b], STEPS_OF_GUESS + 1)
                both(lambda r: nc.vector.tensor_scalar(work[:, r, :], sim[:, t + r, :], guess[:, t + r:t + r + 1], None,
                                                       ALU.is_ge, ALU.add, accum_out=above[:, t + r:t + r + 1]),
                     lambda r: nc.vector.scalar_tensor_tensor(work[:, r, :], work[:, r, :], -3e38, sim[:, t + r, :],
                                                              ALU.mult, ALU.add),
                     lambda r: nc.vector.max(top[:, t + r, 0:8], work[:, r, :]),
                     lambda r: nc.vector.match_replace(work[:, r, :], top[:, t + r, 0:8], work[:, r, :], LOWEST),
                     lambda r: nc.vector.max(top[:, t + r, 8:WINDOW], work[:, r, :]))

            def choose():
                nc.vector.tensor_scalar(wanted[:], above[:], -1.0, KTOP - 1.0, ALU.mult, ALU.add).then_inc(dve_step, 1)
                nc.vector.tensor_scalar(off[:], above[:], 1.0, -COUNT_MID, ALU.mult, ALU.add).then_inc(dve_step, 1)
                steps[0] += 2
                dve.wait_ge(dve_step, steps[0])
                step(nc.vector.tensor_tensor(off_squared[:], off[:], off[:], ALU.mult))
                step(nc.vector.tensor_scalar(missed[:], off_squared[:], (WINDOW / 2) ** 2, None, ALU.is_gt, ALU.add,
                                             accum_out=missed_sum[:]))
                nc.vector.sem_inc(missed_ready, 1)
                for j in range(NT):
                    nc.vector.scalar_tensor_tensor(chosen[:, j, :], iota_lo[:, 0:WINDOW], wanted[:, j:j + 1],
                                                   top[:, j, :], ALU.is_equal, ALU.mult,
                                                   accum_out=threshold[:, j:j + 1]).then_inc(dve_step, 1)
                steps[0] += NT
                dve.wait_ge(dve_step, steps[0])

            def thresholds_in_general():
                per_tile = 2 * ROUNDS + 1
                dve.sem_inc(general_step, 1)
                with dve.Fori(0, NT) as j:
                    count = [per_tile * j + 1]

                    def in_turn():
                        dve.wait_ge(general_step, count[0])
                        own_instruction(dve)
                        count[0] = count[0] + 1

                    in_turn()
                    nc.vector.tensor_copy(work1[:], sim[:, bass.ds(j, 1), :].rearrange("p a n -> p (a n)"))\
                      .then_inc(general_step, 1)
                    for i in range(ROUNDS):
                        in_turn()
                        nc.vector.max(top1[:], work1[:]).then_inc(general_step, 1)
                        if i < ROUNDS - 1:
                            in_turn()
                            nc.vector.match_replace(work1[:], top1[:], work1[:], LOWEST).then_inc(general_step, 1)
                    in_turn()
                    last_kept = (KTOP - 1) % 8
                    nc.vector.tensor_copy(threshold[:, bass.ds(j, 1)], top1[:, last_kept:last_kept + 1])\
                      .then_inc(general_step, 1)
                dve.wait_ge(general_step, per_tile * NT + 1)

            def mask(b):
                dve.wait_ge(sig_ready, b + 1)
                for j in range(b * TPB, (b + 1) * TPB):
                    nc.vector.scalar_tensor_tensor(att[:, j, :], sim[:, j, :], threshold[:, j:j + 1],
                                                   att[:, j, :], ALU.is_ge, ALU.mult).then_inc(att_ready, 1)

            def residual(g):
                dve.wait_ge(gamma_parts, 3)
                for b in range(g * BPG, (g + 1) * BPG):
                    j = slice(b * TPB, (b + 1) * TPB)
                    dve.wait_ge(base_ready, TPB * (b + 1))
                    dve.wait_ge(sum_done, b + 1)
                    nc.vector.scalar_tensor_tensor(x2[:, j, :], ps[:, SIM[b], :].rearrange("p (r n) -> p r n", r=TPB),
                                                   g_half[:, 0:1], xs[:, j, :], ALU.mult, ALU.add).then_inc(x2_ready, 1)
                    dve.wait_ge(x2_ready, b + 1)
                    for t in range(b * TPB, (b + 1) * TPB):
                        nc.vector.bn_stats(stats[:, t, :], x2[:, t, :]).then_inc(x2_summed, 1)
                    for t in range(b * TPB, (b + 1) * TPB):
                        dve.wait_ge(x2_summed, t + 1)
                        nc.vector.bn_aggr(mv2[:, t, :], stats[:, t, :]).then_inc(stats2_ready, 1)

            def normalise_last():
                for j in range(NT - TPG, NT):
                    dve.wait_ge(rstd2_ready, (j - (NT - TPG)) // TPB + 1)
                    nc.vector.tensor_scalar(xn[:, j, 0:H], x2[:, j, :], mv2[:, j, 0:1], rstd2[:, j:j + 1],
                                            ALU.subtract, ALU.mult).then_inc(xn_ready_last, 1)

            def pick(g):
                dve.wait_ge(logits_done, g + 1)
                for r in range(TPG):
                    nc.vector.max(lmax[:, g * TPG + r, :], ps[:, LOG[g], r * E:(r + 1) * E]).then_inc(dve_step, 1)
                steps[0] += TPG
                dve.wait_ge(dve_step, steps[0])
                j = slice(g * TPG, (g + 1) * TPG)
                nc.vector.tensor_tensor(diff[:, j], lmax[:, j, 0], lmax[:, j, 1], ALU.subtract).then_inc(diff_ready, 1)
                for r in range(TPG):
                    nc.vector.max_index(lidx[:, g * TPG + r, :], lmax[:, g * TPG + r, :],
                                        ps[:, LOG[g], r * E:(r + 1) * E]).then_inc(dve_step, 1)
                steps[0] += TPG
                dve.wait_ge(dve_step, steps[0])
                dve.wait_ge(const_ready, 1)
                bc = [P, 2, TPG, E]
                step(nc.vector.tensor_tensor(onehot[:, g], iota_e[:, None, None, :].to_broadcast(bc),
                                             lidx[:, j, 0:2].rearrange("p j c -> p c j")[:, :, :, None].to_broadcast(bc), ALU.is_equal))
                nc.vector.tensor_tensor(picked[:, j, :], onehot[:, g, 0], onehot[:, g, 1], ALU.add)\
                  .then_inc(picked_ready, 1)
                dve.wait_ge(prob_ready, 2 * (g + 1))
                step(nc.vector.tensor_tensor(wsel[:], onehot[:, g], prob[:, :, j][:, :, :, None].to_broadcast(bc),
                                             ALU.mult))
                nc.vector.tensor_tensor(xn[:, j, H:ROW], wsel[:, 0], wsel[:, 1], ALU.add).then_inc(row_ready, 1)

            def place(g):
                dve.wait_ge(rank_done, g + 1)
                if g:
                    dve.wait_ge(ids_done, g)
                bc = [P, 2, TPG, E]
                step(nc.vector.tensor_tensor(
                    rsel[:], onehot[:, g],
                    ps[:, LOG[g], RANK_AT:RANK_AT + TPG * E].rearrange("p (r e) -> p r e", e=E)[:, None].to_broadcast(bc), ALU.mult))
                step(nc.vector.tensor_reduce(rank[:], rsel[:], AX.X, ALU.add))
                step(nc.vector.tensor_copy(rank_i[:], rank[:]))
                j = slice(g * TPG, (g + 1) * TPG)
                nc.vector.tensor_single_scalar(hi_i[:], rank_i[:], 7, ALU.arith_shift_right).then_inc(dve_step, 1)
                nc.vector.tensor_single_scalar(lo_i[:], rank_i[:], P - 1, ALU.bitwise_and).then_inc(dve_step, 1)
                steps[0] += 2
                dve.wait_ge(dve_step, steps[0])
                nc.vector.scalar_tensor_tensor(hi_f[:], lidx[:, j, 0:2].rearrange("p j c -> p c j"), float(MAXT),
                                               hi_i[:], ALU.mult, ALU.add)\
                  .then_inc(dve_step, 1)
                nc.vector.tensor_copy(lo_f[:], lo_i[:]).then_inc(dve_step, 1)
                steps[0] += 2
                dve.wait_ge(dve_step, steps[0])
                bl, bh = [P, 2, TPG, P], [P, 2, TPG, E * MAXT]
                nc.vector.tensor_tensor(oh_hi[:], iota_hi[:, None, None, :].to_broadcast(bh),
                                        hi_f[:, :, :, None].to_broadcast(bh), ALU.is_equal).then_inc(dve_step, 1)
                steps[0] += 1
                nc.vector.tensor_tensor(oh_lo[:], iota_lo[:, None, None, :].to_broadcast(bl),
                                        lo_f[:, :, :, None].to_broadcast(bl), ALU.is_equal)
                dve.wait_ge(dve_step, steps[0])
                nc.vector.tensor_tensor(id_hi[:], oh_hi[:], id1[:, None, j, None].to_broadcast(bh),
                                        ALU.mult).then_inc(one_hots_ready, 1)

            dve.wait_ge(m_done, 1)
            nc.vector.tensor_copy(m_sb[:], ps[0:D, PROJ[0], N:N + D]).then_inc(m_ready, 1)
            projected(0)
            for b in range(B):
                if b < B - 1:
                    projected(b + 1)
                sim_statistics(b)
            dve.wait_ge(const_ready, 1)
            dve.wait_ge(x_loaded, 16)
            for j in range(NT):
                nc.vector.bn_stats(stats[:, j, :], xs[:, j, :]).then_inc(dve_step, 1)
            steps[0] += NT
            dve.wait_ge(dve_step, steps[0])
            for j in range(NT):
                nc.vector.bn_aggr(mv1[:, j, :], stats[:, j, :]).then_inc(stats1_ready, 1)
            for b in range(B):
                find_threshold(b)
            choose()
            dve.wait_ge(missed_done, 1)
            nc.vector.tensor_scalar(missed_any[:], ps[:, IDS, 0:1], 1.0, None, ALU.min).then_inc(missed_seen, 1)
            dve.wait_ge(missed_seen, 1)
            missed_rows = dve.value_load(missed_any[0:1, 0:1], min_val=0, max_val=1)
            with dve.If(missed_rows > 0):
                thresholds_in_general()
            for b in range(B):
                mask(b)
            for g in range(NG):
                residual(g)
            normalise_last()
            for g in range(NG):
                pick(g)
                if g < NG - 1:
                    place(g)
            place(NG - 1)
            dve.wait_ge(rank_done, NG)
            step(nc.vector.tensor_copy(counts[:], ps[:, LOG[NG - 1], COUNT_AT:COUNT_AT + E]))
            bc = [P, E, MAXT - 2]
            step(nc.vector.tensor_tensor(over[:], counts[:, :, None].to_broadcast(bc),
                                         lim[:, None, 2:MAXT].to_broadcast(bc), ALU.is_gt))
            step(nc.vector.tensor_reduce(extra[:], over[:], AX.X, ALU.add))
            dve.wait_ge(ids_done, NG)
            nc.vector.tensor_scalar(idm[:], ps[:, IDS, 0:E * MAXT], -1.0, 0.0, ALU.add, ALU.max).then_inc(dve_step, 1)
            nc.vector.tensor_scalar(pad[:], ps[:, IDS, 0:E * MAXT], 0.0, SKIP, ALU.is_equal, ALU.mult)\
              .then_inc(dve_step, 1)
            steps[0] += 2
            dve.wait_ge(dve_step, steps[0] - 1)
            nc.vector.tensor_copy(gather_ids[:, 0:E * MAXT], idm[:]).then_inc(gather_listed, 1)
            dve.wait_ge(dve_step, steps[0])
            nc.vector.tensor_tensor(scatter_ids[:, MAXT:MAXT + E * MAXT], idm[:], pad[:], ALU.add).then_inc(lists_ready, 1)
            step(nc.vector.memset(extra_before[:, 0, 0:1], 0.0))
            step(nc.vector.tensor_copy(extra_before[:, 0, 1:E], extra[:, 0:E - 1]))
            last_sum = 0
            for span in (1, 2, 4):
                was, now = extra_before[:, last_sum, :], extra_before[:, 1 - last_sum, :]
                nc.vector.tensor_copy(now[:, 0:span], was[:, 0:span]).then_inc(dve_step, 1)
                nc.vector.tensor_tensor(now[:, span:E], was[:, span:E], was[:, 0:E - span], ALU.add).then_inc(dve_step, 1)
                steps[0] += 2
                dve.wait_ge(dve_step, steps[0])
                last_sum = 1 - last_sum
            step(nc.vector.scalar_tensor_tensor(control[:], extra_before[:, last_sum, :], float(MAXT), extra[:],
                                                ALU.mult, ALU.add))
            nc.vector.tensor_copy(ctl[:], control[:]).then_inc(lists_ready, 1)
            dve.wait_ge(lists_ready, 2)

            def x_lo(t, n, slot, e):
                dve.wait_ge(t.x_hi_ready, after(n + 1))
                nc.vector.tensor_copy(t.weight[slot][:], t.xg[slot][:, bass.ds(H + e, 1)]).then_inc(t.weight_ready, 1)
                nc.vector.tensor_tensor(t.xt_lo[:], ps[:, XB, 0:H].rearrange("p (k t) -> p k t", k=KC),
                                        t.xt_hi[:].bitcast(F32), ALU.subtract).then_inc(t.x_ready, 1)

            def hidden(t, n, c):
                dve.wait_ge(t.silu_ready[c], after(n + 1))
                dve.wait_ge(t.h_transposed[1], after(n))
                last = nc.vector.tensor_tensor(t.h[:, c * FCH:(c + 1) * FCH], silu[c][:], ps[:, UB[c], 0:FCH], ALU.mult)
                if c == 1:
                    first, there = FCH - FREST, (FB - 1) * P + REST2
                    last = nc.vector.tensor_tensor(t.h[:, there:there + FREST], silu[c][:, first:FCH],
                                                   ps[:, UB[c], first:FCH], ALU.mult)
                last.then_inc(t.h_ready[c], 1)

            def ht_low(t, n):
                for i, (f0, f1) in enumerate(((0, 4), (4, FB))):
                    dve.wait_ge(t.ht_hi_ready[i], after(n + 1))
                    nc.vector.tensor_tensor(ht_lo[:, f0:f1, :],
                                            ps[:, TB[i], 0:(f1 - f0) * P].rearrange("p (f t) -> p f t", t=P),
                                            ht_hi[:, f0:f1, :].bitcast(F32), ALU.subtract).then_inc(t.ht_ready[i], 1)

            def weigh(t, n, slot, later, listed):
                dve.wait_ge(t.down_done, after(n + 1))
                dve.wait_ge(later.to_listed, after(listed))
                nc.vector.tensor_scalar(t.y[:], ps[:, YB, 0:H], t.weight[slot][:, 0:1], None,
                                        ALU.mult).then_inc(t.y_ready, 1)

            def expert(q, s, last):
                e = 2 * q + s
                extras, so_far = load_control(dve, e)

                def split_next(*pieces):
                    if last:
                        return
                    for i in pieces:
                        dve.wait_ge(w_hi_ready[1 - s], len(PIECES) * (q + s) + i + 1)
                        split = split_low(nc.vector, 1 - s, i)
                        if i == len(PIECES) - 1:
                            split = split_low_rest(nc.vector, 1 - s)
                        split.then_inc((w_lo_gu if i < len(GU_PIECES) else w_lo_d)[1 - s], 1)

                hidden(A, e, 0)
                x_lo(Bc, e, s, e)
                if s == 0:
                    with dve.If(q > 0):
                        ht_low(Bc, e - 1)
                else:
                    ht_low(Bc, e - 1)
                hidden(A, e, 1)
                split_next(1)

                def weigh_b():
                    if s == 0:
                        with dve.If(q > 0):
                            weigh(Bc, e - 1, 1 - s, A, e)
                    else:
                        weigh(Bc, e - 1, 1 - s, A, e)

                with dve.If(extras > 0):
                    n = so_far
                    x_lo(C, n, 0, e)
                    weigh_b()
                    ht_low(A, e)
                    hidden(C, n, 0)
                    weigh(A, e, s, Bc, e)
                    split_next(2)
                    hidden(C, n, 1)
                    if not last:
                        x_lo(A, e + 1, 1 - s, e + 1)
                    hidden(Bc, e, 0)
                    ht_low(C, n)
                    split_next(3)
                    hidden(Bc, e, 1)
                    weigh(C, n, 0, Bc, e)
                with dve.Else():
                    weigh_b()
                    ht_low(A, e)
                    if not last:
                        x_lo(A, e + 1, 1 - s, e + 1)
                    split_next(2)
                    hidden(Bc, e, 0)
                    split_next(3)
                    if last:
                        hidden(Bc, e, 1)
                    weigh(A, e, s, Bc, e)
                    if not last:
                        hidden(Bc, e, 1)
                split_next(5)
                with dve.If(extras > 1):
                    with dve.Fori(1, extras) as t:
                        n = so_far + t
                        x_lo(C, n, 0, e)
                        hidden(C, n, 0)
                        hidden(C, n, 1)
                        ht_low(C, n)
                        weigh(C, n, 0, C, n + 1)

            x_lo(A, 0, 0, 0)
            with dve.Fori(0, E // 2 - 1) as q:
                expert(q, 0, False)
                expert(q, 1, False)
            expert(E // 2 - 1, 0, False)
            expert(E // 2 - 1, 1, True)
            ht_low(Bc, E - 1)
            weigh(Bc, E - 1, 1, A, E)

        @block.gpsimd
        def _(pool):
            steps = [0]

            def step(ins):
                steps[0] += 1
                ins.then_inc(pool_step, 1)
                pool.wait_ge(pool_step, steps[0])

            nc.gpsimd.memset(ones_f[:], 1.0).then_inc(const_step, 1)
            nc.gpsimd.memset(ones_h[:], 1.0).then_inc(const_step, 1)
            nc.gpsimd.memset(minus_half[:], -0.5).then_inc(const_step, 1)
            nc.gpsimd.memset(half[:], 0.5).then_inc(const_step, 1)
            pool.wait_ge(const_step, 4)
            nc.gpsimd.affine_select(out=ident[:], in_=ones_f[:], compare_op=ALU.is_equal, fill=0.0, base=0,
                                    pattern=[[-1, P]], channel_multiplier=1).then_inc(const_step, 1)
            nc.gpsimd.affine_select(out=earlier[:], in_=ones_h[:], compare_op=ALU.is_gt, fill=0.0, base=0,
                                    pattern=[[1, P]], channel_multiplier=-1).then_inc(const_step, 1)
            imprecise = dict(allow_small_or_imprecise_dtypes=True)
            nc.gpsimd.iota(iota_e[:], pattern=[[1, E]], base=0, channel_multiplier=0, **imprecise).then_inc(const_step, 1)
            nc.gpsimd.iota(iota_lo[:], pattern=[[1, P]], base=0, channel_multiplier=0, **imprecise).then_inc(const_step, 1)
            nc.gpsimd.iota(iota_hi[:], pattern=[[1, E * MAXT]], base=0, channel_multiplier=0, **imprecise)\
              .then_inc(const_step, 1)
            nc.gpsimd.iota(id1[:], pattern=[[P, NT]], base=1, channel_multiplier=1, **imprecise).then_inc(const_step, 1)
            nc.gpsimd.iota(lim[:], pattern=[[P, MAXT]], base=0, channel_multiplier=0, **imprecise).then_inc(const_step, 1)
            pool.wait_ge(const_step, 11)
            pool.sem_inc(const_ready, 1)

            def first_guess(b):
                t = slice(b * TPB, (b + 1) * TPB)
                pool.wait_ge(sim_stats, TPB * (b + 1))
                step(nc.gpsimd.tensor_tensor(deviation[:, t], mvs[:, t, 1], half[:, t], ALU.pow))
                step(nc.gpsimd.tensor_tensor(move[:, t], deviation[:, t], half[:, t], ALU.mult))
                step(nc.gpsimd.tensor_tensor(guess[:, t], move[:, t], mvs[:, t, 0], ALU.add))
                pool.sem_inc(guess_ready[b], 1)
                nc.gpsimd.tensor_scalar(slope[:, t], deviation[:, t], -0.5 / GUESS_DENSITY, 0.0, ALU.mult, ALU.add)\
                  .then_inc(pool_step, 1)
                nc.gpsimd.tensor_scalar(slope_base[:, t], deviation[:, t], (N / 2 - TARGET) / GUESS_DENSITY, 0.0,
                                        ALU.mult, ALU.add).then_inc(pool_step, 1)
                steps[0] += 2
                pool.wait_ge(pool_step, steps[0])
                nc.gpsimd.tensor_tensor(guess_base[:, t], guess[:, t], slope_base[:, t], ALU.add)\
                  .then_inc(pool_step, 1)
                steps[0] += 1

            def next_guess(b, i):
                t = slice(b * TPB, (b + 1) * TPB)
                pool.wait_ge(pool_step, steps[0])
                step(nc.gpsimd.tensor_tensor(move[:, t], signs[:, t], slope[:, t], ALU.mult))
                step(nc.gpsimd.tensor_tensor(guess[:, t], move[:, t], guess_base[:, t], ALU.add))
                pool.sem_inc(guess_ready[b], 1)
                if i < STEPS_OF_GUESS - 1:
                    nc.gpsimd.tensor_tensor(guess_base[:, t], guess[:, t], slope_base[:, t], ALU.add)\
                      .then_inc(pool_step, 1)
                    steps[0] += 1

            first_guess(0)
            for at, (b, i) in enumerate(passes):
                pool.wait_ge(signs_counted, TPB * (at + 1))
                next_guess(b, i)
                if at in (0, 3, 4):
                    first_guess({0: 1, 3: 2, 4: 3}[at])
            pool.wait_ge(gamma_ready, 1)
            nc.gpsimd.tensor_scalar(g_half[:], g_full[:], 0.5, 0.0, ALU.mult, ALU.add).then_inc(gamma_parts, 1)
            nc.gpsimd.tensor_scalar(g_rest[:], g_full[:], -1.0, 1.0, ALU.mult, ALU.add).then_inc(gamma_parts, 1)
            nc.gpsimd.tensor_scalar(g_neg[:], g_full[:], 1.0, -1.0, ALU.mult, ALU.add).then_inc(gamma_parts, 1)
            pool.wait_ge(stats1_ready, NT)
            pool.wait_ge(gamma_parts, 3)
            step(nc.gpsimd.tensor_scalar(ve[:], mv1[:, :, 1], 1.0, EPS, ALU.mult, ALU.add))
            step(nc.gpsimd.tensor_tensor(rstd[:], ve[:], minus_half[:], ALU.pow))
            nc.gpsimd.tensor_scalar(ln_scale[:], rstd[:], g_rest[:, 0:1], 1.0, ALU.mult, ALU.add).then_inc(ln1_ready, 1)
            step(nc.gpsimd.tensor_tensor(lnb[:], rstd[:], mv1[:, :, 0], ALU.mult))
            nc.gpsimd.tensor_scalar(ln_bias[:], lnb[:], g_neg[:, 0:1], 0.0, ALU.mult, ALU.add).then_inc(ln1_ready, 1)

            def split_lo(slot, uses, i):
                pool.wait_ge(w_hi_ready[slot], len(PIECES) * uses + i + 1)
                done = (w_lo_gu if i < len(GU_PIECES) else w_lo_d)[slot]
                if i < len(PIECES) - 1:
                    split_low(nc.gpsimd, slot, i).then_inc(done, 1)
                else:
                    step(split_low(nc.gpsimd, slot, i))
                    step(split_low_rest(nc.gpsimd, slot))
                    pool.sem_inc(done, 1)

            for i in range(len(PIECES)):
                split_lo(0, 0, i)
            parts = [(g * TPG, (g + 1) * TPG) for g in range(NG - 1)]
            parts += [(b * TPB, (b + 1) * TPB) for b in range(B - BPG, B)]
            for first, end in parts:
                j = slice(first, end)
                pool.wait_ge(stats2_ready, end)
                step(nc.gpsimd.tensor_scalar(ve2[:, j], mv2[:, j, 1], 1.0, EPS, ALU.mult, ALU.add))
                power = nc.gpsimd.tensor_tensor(rstd2[:, j], ve2[:, j], minus_half[:, j], ALU.pow)
                if first < NT - TPG:
                    step(power)
                    step(nc.gpsimd.tensor_tensor(nm2[:, j], rstd2[:, j], mv2[:, j, 0], ALU.mult))
                    nc.gpsimd.tensor_scalar(nmr2[:, j], nm2[:, j], -1.0, 0.0, ALU.mult, ALU.add).then_inc(ln2_ready, 1)
                else:
                    power.then_inc(rstd2_ready, 1)
            pool.dma_start(out_view[:, NT - TPG:NT, :], x2[:, NT - TPG:NT, :]).then_inc(landed, 16)

            def gather(t, n, e, tile, slot):
                own_instruction(pool)
                nc.gpsimd.tensor_copy(t.from_rows[slot][:], gather_ids[:, bass.ds(e * MAXT + tile, 1)])\
                  .then_inc(t.from_listed, 1)
                pool.wait_ge(t.from_listed, after(n + 1))
                own_instruction(pool)
                pool.indirect_dma_start(out=t.xg[slot][:], out_offset=None, in_=scratch,
                                        in_offset=bass.IndirectOffsetOnAxis(ap=t.from_rows[slot][:], axis=0))\
                    .then_inc(t.gathered[slot], 16)

            def scatter(t, n, e, tile, scatters_before):
                pool.wait_ge(landed, 16 * (scatters_before + 1))
                own_instruction(pool)
                nc.gpsimd.tensor_copy(t.to_rows[:], scatter_ids[:, bass.ds((e + 1) * MAXT + tile, 1)])\
                  .then_inc(t.to_listed, 1)
                pool.wait_ge(t.to_listed, after(n + 1))
                pool.wait_ge(t.y_ready, after(n + 1))
                own_instruction(pool)
                pool.indirect_dma_start(out=out_rows, in_=t.y[:], in_offset=None,
                                        out_offset=bass.IndirectOffsetOnAxis(ap=t.to_rows[:], axis=0),
                                        bounds_check=TOK - 1, oob_is_err=False, compute_op=ALU.add)\
                    .then_inc(landed, 16)

            pool.wait_ge(gather_listed, 1)
            pool.wait_ge(rows_stored, 16 * NG)
            gather(A, 0, 0, 0, 0)
            gather(Bc, 0, 0, 1, 0)
            pool.wait_ge(lists_ready, 2)
            first_extras, _ = load_control(pool, 0)
            with pool.If(first_extras > 0):
                gather(C, 0, 0, 2, 0)
            pool.wait_ge(x2_stored, 16 * (NG - 1))
            pool.wait_ge(landed, 16)

            def expert(q, s, last):
                e = 2 * q + s
                extras, so_far = load_control(pool, e)
                if not last:
                    next_extras, next_so_far = load_control(pool, e + 1)
                    gather(A, e + 1, e + 1, 0, 1 - s)
                    pool.wait_ge(Bc.weight_ready, after(e))
                    gather(Bc, e + 1, e + 1, 1, 1 - s)

                def previous_b():
                    split_lo(s, q, 4)
                    scatter(Bc, e - 1, e - 1, 1, 2 * e - 1 + so_far)

                if s == 0:
                    with pool.If(q > 0):
                        previous_b()
                else:
                    previous_b()

                def next_c():
                    with pool.If(next_extras > 0):
                        pool.wait_ge(C.weight_ready, after(next_so_far))
                        gather(C, next_so_far, e + 1, 2, 0)

                if not last:
                    split_lo(1 - s, q + s, 0)
                    with pool.If(extras < 2):
                        next_c()
                scatter(A, e, e, 0, 2 * e + so_far)
                with pool.If(extras > 0):
                    scatter(C, so_far, e, 2, 2 * e + 1 + so_far)
                with pool.If(extras > 1):
                    with pool.Fori(1, extras) as t:
                        n = so_far + t
                        pool.wait_ge(C.weight_ready, after(n))
                        gather(C, n, e, 2 + t, 0)
                        scatter(C, n, e, 2 + t, 2 * e + 1 + n)
                    if not last:
                        next_c()

            with pool.Fori(0, E // 2 - 1) as q:
                expert(q, 0, False)
                expert(q, 1, False)
            expert(E // 2 - 1, 0, False)
            expert(E // 2 - 1, 1, True)
            extras, so_far = load_control(pool, E - 1)
            scatter(Bc, E - 1, E - 1, 1, 2 * E - 1 + so_far + extras)
            pool.wait_ge(landed, 16 * (2 * E + so_far + extras + 1))
            own_instruction(pool)


def kernel(**inputs):
    import numpy as np
    import concourse.bacc as bacc
    from concourse import mybir as my
    from concourse.bass_utils import run_bass_kernel_spmd as run

    a = {k: np.asarray(v) for k, v in inputs.items()}
    e, f, h = a["L0_ffn_gate_w"].shape
    kc = h // 128
    whole = f // 128 * 128
    down_t = a["L0_ffn_down_w"].transpose(0, 2, 1)

    def contraction_first(w):
        return w.reshape(e, f, kc, 128).transpose(0, 3, 2, 1).reshape(e, 128, kc * f)

    laid_out = {
        "x": a["x"],
        "ctxT": a["ctx_512"].reshape(-1, a["ctx_512"].shape[-1]).T,
        "wq": a["L0_xattn_Wq"],
        "wk": a["L0_xattn_Wk"],
        "gamma": a["L0_xattn_gamma_raw"].reshape(1),
        "routerT": a["L0_ffn_router_w"].reshape(e, kc, 128).transpose(2, 1, 0),
        "gate": contraction_first(a["L0_ffn_gate_w"]),
        "up": contraction_first(a["L0_ffn_up_w"]),
        "down": down_t[:, :whole].reshape(e, whole // 128, 128, h).transpose(0, 2, 1, 3).reshape(e, 128, -1),
        "down_rest": down_t[:, whole:],
    }
    nc = bacc.Bacc("TRN2", target_bir_lowering=False, num_devices=1)
    arrays, args = {}, []
    for name, v in laid_out.items():
        v = np.ascontiguousarray(v)
        arrays[f"in_{name}"] = v
        args.append(nc.dram_tensor(f"in_{name}", v.shape, my.dt.from_np(v.dtype), kind="ExternalInput").ap())
    args.append(nc.dram_tensor("out_0", a["x"].shape, my.dt.from_np(a["x"].dtype), kind="ExternalOutput").ap())
    xattn_moe_kernel(nc, *args)
    return run(nc, [arrays], core_ids=[0]).results[0]["out_0"]
```
